# Optimizing a Trainium2 kernel written in Bass

```python
import numpy as np
import jax
import jax.numpy as jnp

def _softmax(x, axis=-1):
    return jax.nn.softmax(x, axis=axis)

def _gelu(x):
    return jax.nn.gelu(x, approximate=True)

def _silu(x):
    return jax.nn.silu(x)

def _sigmoid(x):
    return jax.nn.sigmoid(x)

def _layernorm(x, axis=-1, eps=1e-05):
    m = jnp.mean(x, axis=axis, keepdims=True)
    v = jnp.var(x, axis=axis, keepdims=True)
    return (x - m) / jnp.sqrt(v + eps)

def _scatter_add(tgt, idx, src, axis=0):
    return tgt.at[idx].add(src)

def _segment_sum(src, seg, n):
    return jax.ops.segment_sum(src, seg, n)
kernel_name = 'mk_gnn_ffn_d1_gnn_r8_b1418f'

def setup_inputs(seed: int=0):
    np.random.seed(seed)
    _w = jnp.asarray

    def _rec_inputs():
        import jax
        import jax.numpy as jnp
        _gk = jax.random.key(seed)
        x = -7.329e-05 + 0.9999 * jax.random.normal(jax.random.fold_in(_gk, 1), (1250, 1024), jnp.float32)
        _s = jax.random.randint(jax.random.fold_in(_gk, 2), (10000,), 0, 1250, jnp.int32)
        _d = jax.random.randint(jax.random.fold_in(_gk, 3), (10000,), 0, 1250, jnp.int32)
        _loop = jnp.arange(1250, dtype=jnp.int32)
        src = jnp.concatenate([_s, _d, _loop])
        dst = jnp.concatenate([_d, _s, _loop])
        _o = jnp.argsort(dst, stable=True)
        src = src[_o]
        dst = dst[_o]
        edge_weight = -0.000130211 + 0.031236 * jax.random.normal(jax.random.fold_in(_gk, 12), (21250,), jnp.float32)
        return (x, src, dst, edge_weight)
    x, src, dst, edge_weight = _rec_inputs()

    def _L0_gnn_setup():
        import jax, jax.numpy as jnp
        import numpy as np
        INDIM = 1024
        OUTDIM = 1024
        NNZ = 8192
        N = 6250
        key = jax.random.key(seed)
        k1, k2, k3, k4, k5 = jax.random.split(key, 5)
        x = jax.random.normal(k1, (N, INDIM), dtype=jnp.float32)
        stdv = np.sqrt(6.0 / (INDIM + OUTDIM))
        nnz_weight = jax.random.uniform(k2, (NNZ,), dtype=jnp.float32, minval=-stdv, maxval=stdv)
        bias = jax.random.normal(k3, (OUTDIM,), dtype=jnp.float32) * 0.02
        row = jax.random.randint(k4, (NNZ,), 0, OUTDIM, dtype=jnp.int64)
        col = jax.random.randint(k5, (NNZ,), 0, INDIM, dtype=jnp.int64)
        edge_index = jnp.stack([row, col])
        return {'x': x, 'nnz_weight': nnz_weight, 'bias': bias, 'edge_index': edge_index}
    _L0_gnn_all = _L0_gnn_setup()
    _L0_gnn_in = {k: v for k, v in _L0_gnn_all.items() if k in ('bias',)}
    del _L0_gnn_all

    def _L0_ffn_setup():
        import jax, jax.numpy as jnp
        import numpy as np
        TOP_K = 2
        key = jax.random.key(seed)
        ks = jax.random.split(key, 6)
        B, T, H, E, F = (2, 256, 1024, 8, 512)
        s = 0.02
        return {'hidden_states': jax.random.normal(ks[0], (B, T, H), dtype=jnp.float32), 'router_w': jax.random.normal(ks[1], (E, H), dtype=jnp.float32) * s, 'w1': jax.random.normal(ks[2], (E, F, H), dtype=jnp.float32) * s, 'b1': jax.random.normal(ks[3], (E, F), dtype=jnp.float32) * s, 'w2': jax.random.normal(ks[4], (E, H, F), dtype=jnp.float32) * s, 'b2': jax.random.normal(ks[5], (E, H), dtype=jnp.float32) * s}
    _L0_ffn_all = _L0_ffn_setup()
    _L0_ffn_in = {k: v for k, v in _L0_ffn_all.items() if k in ('router_w', 'w1', 'b1', 'w2', 'b2')}
    del _L0_ffn_all
    return {'x': x, 'src': src, 'dst': dst, 'edge_weight': edge_weight, 'L0_gnn_bias': _L0_gnn_in['bias'], 'L0_ffn_router_w': _L0_ffn_in['router_w'], 'L0_ffn_w1': _L0_ffn_in['w1'], 'L0_ffn_b1': _L0_ffn_in['b1'], 'L0_ffn_w2': _L0_ffn_in['w2'], 'L0_ffn_b2': _L0_ffn_in['b2']}

def reference(x, src, dst, edge_weight, L0_gnn_bias, L0_ffn_router_w, L0_ffn_w1, L0_ffn_b1, L0_ffn_w2, L0_ffn_b2):
    import jax
    import jax.numpy as jnp

    def _L0_gnn_ref(x, nnz_weight, bias, edge_index):
        import jax, jax.numpy as jnp
        import numpy as np
        INDIM = 1024
        OUTDIM = 1024
        NNZ = 8192
        N = 6250
        row, col = (edge_index[0], edge_index[1])
        W = jnp.zeros((OUTDIM, INDIM), dtype=nnz_weight.dtype).at[row, col].add(nnz_weight)
        return x @ W.T + bias

    def _L0_ffn_ref(hidden_states, router_w, w1, b1, w2, b2):
        import jax, jax.numpy as jnp
        import numpy as np
        TOP_K = 2
        x = hidden_states
        router_logits = jnp.einsum('bth,eh->bte', x, router_w)
        topk_values, topk_indices = jax.lax.top_k(router_logits, TOP_K)
        topk_weights = jax.nn.softmax(topk_values.astype(jnp.float32), axis=-1).astype(x.dtype)
        h1 = jnp.einsum('bth,efh->btef', x, w1) + b1
        h1 = jax.nn.gelu(h1, approximate=False)
        expert_outputs = jnp.einsum('btef,ehf->bteh', h1, w2) + b2
        gather_idx = topk_indices[..., None]
        topk_expert_outputs = jnp.take_along_axis(expert_outputs, gather_idx, axis=2)
        mixed_output = jnp.sum(topk_expert_outputs * topk_weights[..., None], axis=2)
        return mixed_output
    edge_index = jnp.stack([src, dst])
    x = x + _L0_gnn_ref(_layernorm(x, axis=-1), edge_weight, L0_gnn_bias, edge_index)
    x = x + _L0_ffn_ref(_layernorm(x, axis=-1)[None], L0_ffn_router_w, L0_ffn_w1, L0_ffn_b1, L0_ffn_w2, L0_ffn_b2)[0]
    return x

_drawn_inputs = setup_inputs


def setup_inputs(seed=0):
    import zlib

    import numpy as np

    out = dict(_drawn_inputs(seed))
    spreads = {}
    factors = {'L0_ffn_b1': 8.0, 'L0_ffn_b2': 3.932}
    for name, (base, spread) in spreads.items():
        noise = np.random.default_rng([zlib.crc32(name.encode()), seed]).standard_normal(out[name].shape)
        drawn = base * np.exp(spread * noise) if base else spread * noise
        out[name] = jnp.asarray(drawn.astype(out[name].dtype))
    for name, factor in factors.items():
        out[name] = (out[name] * factor).astype(out[name].dtype)
    return out
```

```python
from contextlib import ExitStack

import concourse.bass as bass
from concourse import mybir

ALU = mybir.AluOpType
ACT = mybir.ActivationFunctionType
AX = mybir.AxisListType
F32 = mybir.dt.float32
F16 = mybir.dt.float16
I32 = mybir.dt.int32
U32 = mybir.dt.uint32

P = 128
N = 1250
D = 1024
KB = D // P
NE = 21250
E = 8
F = 512
FB = F // P
HALF = 512
EPS = 1e-5
SCALE = 64.0
TILES = (N + P - 1) // P
LAST = N - P
REPEAT = P * TILES - N

WIN = 64
WINS = D // WIN
GRP = 4
CHUNKS = (NE + P - 1) // P
NCH = 172
FAR = 2 ** 20
BIG = 512.0

CAP = N // P * P + 2 * P
DUMP = E * CAP
ROW = 2080
GATE = 2 * D
DEST = GATE + 2 * E
TILES_MAX = (2 * N + E * (P - 1)) // P
TMAX = 32
UNITS = 8
RING = 4
MAGIC = 0x5F3759DF

H_ID, H_TRI, H_ONE, H_ONE2, H_IOTA, H_END = 0, 128, 256, 384, 512, 512 + D
S_ID, S_I64, S_I16, S_I8, S_CH, S_EB, S_MASK, S_DUMP, S_IT, S_SC, S_END = (
    0, 128, 192, 208, 216, 220, 228, 238, 258, 290, 291)


class Chain:

    def __init__(self, eng, sem, per):
        self.eng, self.sem, self.per, self.base, self.n = eng, sem, per, 0, 0

    def start(self, index):
        assert self.n in (0, self.per), (self.n, self.per)
        self.base, self.n = index * self.per, 0

    def inc(self, ins):
        self.n += 1
        ins.then_inc(self.sem, 1)

    def link(self, ins):
        self.inc(ins)
        self.eng.wait_ge(self.sem, self.base + self.n)

    def link_apart(self, ins, passed):
        self.link(ins)
        self.eng.sem_inc(passed, 1)


def build_program(nc, x, src, dst, edge_w, bias, router, w1u, w2u, b1, b2, c16, c32, ci, out):
    ctx = ExitStack()
    with ctx:
        def sb(name, shape, dt):
            return ctx.enter_context(nc.sbuf_tensor(name, shape, dt))

        def sem(name):
            return ctx.enter_context(nc.semaphore(name))

        lists = nc.dram_tensor("lists", [DUMP + 2 * P, ROW // 2], I32).ap()
        acc = nc.dram_tensor("acc", [N + P, D], F32).ap()

        k16 = sb("k16", [P, H_END], F16)
        k32 = sb("k32", [P, S_END], F32)
        kdest = sb("kdest", [P, 16], I32)
        slots = sb("slots", [P, 2, 2, UNITS, D], F16)
        wT = slots[:, 1]
        dst1h = slots[:, 0].rearrange("p a b c -> p (a b c)")[:, 0:NCH * WIN].rearrange("p (c n) -> p c n", n=WIN)
        late = sb("late", [P, NCH * 2 * WIN], F16)
        stat = late[:].rearrange("p (c n) -> p c n", n=2 * WIN)
        BCOLS = E * (F + D)
        brow = late[:, 0:BCOLS]
        xs = late[:, BCOLS:BCOLS + 4 * ROW + 0] if BCOLS + 4 * ROW <= NCH * 2 * WIN else None
        assert xs is not None
        xs = xs.rearrange("p (r n) -> p r n", n=ROW)
        staging = sb("staging", [P, RING, D], F32)
        ring1h = sb("ring1h", [P, GRP, D], F16)
        x1 = ring1h[:].rearrange("p r n -> p (r n)").bitcast(F32)[:, 0:2 * D].rearrange("p (r n) -> p r n", n=D)
        xin = sb("xin", [P, 2, D], F32)
        padrows = xin[:].rearrange("p r n -> p (r n)").bitcast(F16)[:, 0:ROW]
        xb = sb("xb", [P, 2, D], F32)
        yout = xb[:, 0]
        hgelu = xb[:, 1, 0:F]
        hsplit = xb[:, 1].bitcast(F16)[:, 2 * F:4 * F].rearrange("p (s n) -> p s n", s=2)
        biasb = sb("biasb", [P, D], F32)
        xln = sb("xln", [P, D], F32)
        xln2 = sb("xln2", [P, D], F32)
        wsum = xln2[:]
        row1 = sb("row1", [P, 2, 2 * D], F16)
        row2 = sb("row2", [P, 2, ROW], F16)
        xTs = sb("xTs", [P, 3, 2, KB, P], F16)
        xT = xTs[:, 0:2]
        x2T = xTs[:, 2]
        srcw = xTs[:].rearrange("p a b c d -> p (a b c d)").bitcast(F32)[:, 0:WINS * NCH].rearrange(
            "p (w c) -> p w c", w=WINS)
        xsT = x2T
        hT = xTs[:, 0]
        edge_i = xln2[:, 0:4 * P].bitcast(I32).rearrange("p (h j e) -> p h j e", h=2, j=2)
        edge_f = xln2[:, 4 * P:6 * P].rearrange("p (h e) -> p h e", h=2)
        tmp_i = xln2[:, 6 * P:8 * P].bitcast(I32).rearrange("p (h e) -> p h e", h=2)
        quant = sb("quant", [P, 2, 4, P], F32)
        eT = sb("eT", [P, 4, 2 * P], F32)
        whi16 = sb("whi16", [P, 2 * P], F16)
        whl = sb("whl", [P, 2, 2 * P], F32)
        bmm = sb("bmm", [P, 2, 2], F32)
        touch = sb("touch", [P, 2, 2, WINS], F32)
        lohi = sb("lohi", [P, 2 * WINS], F32)
        lohiT = sb("lohiT", [2 * WINS, 1], F32)
        wrow = sb("wrow", [1, 6, WINS], F32)
        wtab = sb("wtab", [1, 5, WINS], I32)
        wlow = row2[0:WIN, 1, 0:2 * D].bitcast(F32)
        brow12 = row2[0:12, 0, 0:2 * D].bitcast(F32)
        b12 = eT[0:12].rearrange("p q n -> p (q n)").bitcast(F16).rearrange("p (a n) -> p a n", a=2)
        rw = sb("rw", [P, KB, E], F32)
        rws = sb("rws", [P, KB, 2 * E], F16)
        st1 = sb("st1", [P, 2, 6], F32)
        mv1 = sb("mv1", [P, 8], F32)
        ab1 = sb("ab1", [P, 2, 2], F32)
        st2 = sb("st2", [P, 2, 6], F32)
        mv2 = sb("mv2", [P, 8], F32)
        ab2 = sb("ab2", [P, 2, 2], F32)
        logit = sb("logit", [P, 2, E], F32)
        m8 = sb("m8", [P, 8], F32)
        i8 = sb("i8", [P, 8], U32)
        idf = sb("idf", [P, 2], F32)
        nb = sb("nb", [P, 1], F32)
        ex = sb("ex", [P, 1], F32)
        gs = sb("gs", [P, 4], F32)
        pick = sb("pick", [P, 3, E], F32)
        mk = sb("mk", [P, 2, E], F16)
        mcum = sb("mcum", [P, 2, E], F16)
        pos = sb("pos", [P, 3, E], F32)
        slotf = sb("slotf", [P, 2], F32)
        slot_i = sb("slot_i", [P, 2, 2], I32)
        cnts = sb("cnts", [1, 6, E], F32)
        cnti = sb("cnti", [1, 4, E], I32)
        tt = quant[0:1].rearrange("p h q n -> p (h q n)")[:, 0:2 * TMAX * E].rearrange("p (a i e) -> p a i e", a=2, e=E)
        tf = sb("tf", [1, 6, TMAX], F32)
        ftab = sb("ftab", [1, 3, TMAX], I32)
        fmisc = sb("fmisc", [1, 3, E], I32)
        dest_i = sb("dest_i", [P, 1], I32)
        gate_f = sb("gate_f", [P, 1], F32)

        psA = ctx.enter_context(nc.psum_tensor("psA", [P, 2, HALF], F32))
        psT = ctx.enter_context(nc.psum_tensor("psT", [P, 2, KB, P], F16))
        psW = ctx.enter_context(nc.psum_tensor("psW", [P, 4, HALF], F32))
        psR = psW[:, 0]
        psK = psW[:, 1]
        psH = psW[:, 2]
        psHT = psW[:, 3].bitcast(F16).rearrange("p (s f n) -> p s f n", s=2, f=FB)

        s = {}
        for name in """consts_in edges_in biases_in brow_in bcast_in pads_set brow_zero quant_done edges_turned
                       parts_done dst1h_done wtab_done range_turned range_done range_row stat_done group_done
                       win_merged odd_scaled dve_passed pool_passed act_passed low_brought wsplit_done xln_done hi1_done lo1_done xb_done stats1_done t1_done t1_copied
                       gnn_done x1_done stats2_done xln2_done hi2_done lo2_done t2_done t2_copied router_done
                       nb_done exp_done gate_done mask_done rank_done slot_done count_done table_done rws_done
                       padrow_done pads_out b12_done b12_lo mcum_zero rowpad_done wsplit_hi
                       lo_even lo_odd hi_done xs_in xs_done l1_done gelu_done hhi_done hlo_done ht_done ht_copied l2_done
                       y_done dest_done y_added out_done acc_pad gatec_done
                       xsT_copied gates_built c_dest c_edge c_rng c_ln1 c_ln2 c_rt c_rk c_tab c_row""".split():
            s[name] = sem(name)
        S = s
        src1h_ready = [sem(f"src1h_ready{g}") for g in range(GRP)]
        src1h_used = [sem(f"src1h_used{g}") for g in range(GRP)]
        x_in = [sem(f"x_in{h}") for h in range(2)]
        x1_out = [sem(f"x1_out{h}") for h in range(2)]
        listed = [sem(f"listed{h}") for h in range(2)]
        unit_in = [sem(f"unit_in{r}") for r in range(RING)]

        ident = k16[:, H_ID:H_ID + P]
        tri = k16[:, H_TRI:H_TRI + P]
        ones = k16[:, H_ONE:H_ONE + P]
        ones2 = k16[:, H_ONE2:H_ONE2 + P]
        iota1 = k16[:, H_IOTA:H_IOTA + D]
        scale_col = k32[:, S_SC:S_SC + 1]
        ident32 = k32[:, S_ID:S_ID + P]

        def tile_start(t):
            return P * t - REPEAT * (t // (TILES - 1))

        def tiles(body, eng):
            body(0, 0)
            body(1, 1)
            with eng.Fori(1, TILES // 2 - 1) as i:
                body(2 * i, 0)
                body(2 * i + 1, 1)
            body(TILES - 2, 0)
            body(TILES - 1, 1)

        def within(v, low, high):
            return v if isinstance(v, int) else v.with_bounds(min_val=low, max_val=high)

        def known(t, low):
            return t >= low if isinstance(t, int) else True

        def below(t, high):
            return t < high if isinstance(t, int) else True

        block = ctx.enter_context(nc.Block())

        @block.sync
        def _(sp):
            full = NE // P - P
            rest = NE - (P + full) * P
            sp.dma_start(k32[:], c32).then_inc(S["consts_in"], 16)
            for j, a in enumerate((src, dst)):
                sp.dma_start(edge_i[:, 0, j, :], a[0:P * P].rearrange("(c e) -> c e", e=P)).then_inc(S["edges_in"], 16)
            sp.dma_start(edge_f[:, 0, :], edge_w[0:P * P].rearrange("(c e) -> c e", e=P)).then_inc(S["edges_in"], 16)
            sp.wait_ge(S["pads_set"], 1)
            for j, a in enumerate((src, dst)):
                sp.dma_start(edge_i[0:full, 1, j, :],
                             a[P * P:(P + full) * P].rearrange("(c e) -> c e", e=P)).then_inc(S["edges_in"], 16)
                sp.dma_start(edge_i[full:full + 1, 1, j, 0:rest],
                             a[(P + full) * P:NE].rearrange("(c e) -> c e", c=1)).then_inc(S["edges_in"], 16)
            sp.dma_start(edge_f[0:full, 1, :],
                         edge_w[P * P:(P + full) * P].rearrange("(c e) -> c e", e=P)).then_inc(S["edges_in"], 16)
            sp.dma_start(edge_f[full:full + 1, 1, 0:rest],
                         edge_w[(P + full) * P:NE].rearrange("(c e) -> c e", c=1)).then_inc(S["edges_in"], 16)
            sp.dma_start(k16[:], c16).then_inc(S["consts_in"], 16)
            sp.dma_start(kdest[:], ci).then_inc(S["consts_in"], 16)
            for h in range(2):
                sp.dma_start(xin[:, h, :], x[h * P:(h + 1) * P, :]).then_inc(x_in[h], 16)
            sp.dma_start(biasb[:], bias.to_broadcast([P, D])).then_inc(S["bcast_in"], 16)
            sp.dma_start(rw[:], router).then_inc(S["biases_in"], 16)
            sp.dma_start(brow12[0:4, :], b1).then_inc(S["biases_in"], 16)
            sp.dma_start(brow12[4:12, :], b2).then_inc(S["biases_in"], 16)
            for r in range(RING):
                sp.dma_start(staging[:, r, :], w1u[r, :, :]).then_inc(unit_in[r], 16)

            def gnn_tile(t, h):
                if below(t, TILES - 2):
                    sp.wait_ge(S["xb_done"], t + 1)
                    sp.wait_ge(S["xln_done"], t + 1)
                    sp.dma_start(xin[:, h, :], x[bass.ds(tile_start(t + 2), P), :]).then_inc(x_in[h], 16)
                if isinstance(t, int) and t == TILES - 1:
                    sp.wait_ge(x1_out[1 - h], 16 * (TILES // 2))
                sp.wait_ge(S["x1_done"], t + 1)
                sp.dma_start(acc[bass.ds(tile_start(t), P), :], x1[:, h, :]).then_inc(x1_out[h], 16)

            for t in range(TILES):
                if 4 <= t < 4 + RING:
                    r = t - 4
                    sp.wait_ge(S["lo_odd"] if r % 2 else S["lo_even"], r // 2 + 1)
                    sp.dma_start(staging[:, r, :], w2u[r, :, :]).then_inc(unit_in[r], 16)
                gnn_tile(t, t % 2)
            sp.wait_ge(S["table_done"], 1)
            sp.wait_ge(S["padrow_done"], 1)
            with sp.Fori(0, E) as e:
                first = sp.value_load(fmisc[0:1, 0, bass.ds(e, 1)], min_val=0, max_val=E * CAP - P)
                sp.dma_start(lists[bass.ds(first, P), :], padrows.bitcast(I32)).then_inc(S["pads_out"], 16)
            sp.wait_ge(S["brow_zero"], 1)
            sp.wait_ge(S["b12_lo"], 1)
            for j in range(2):
                sp.dma_start(brow[32 * j:32 * j + 1, :].rearrange("o (r n) -> o r n", n=D), b12[:, j, :]
                             ).then_inc(S["brow_in"], 16)
            with sp.Fori(1, E) as e:
                for u in range(UNITS):
                    r = u % RING
                    sp.wait_ge(S["lo_odd"] if r % 2 else S["lo_even"], 4 * e + u // 2 - 1)
                    w = w1u if u < 4 else w2u
                    sp.dma_start(staging[:, r, :], w[bass.ds(4 * e + u % 4, 1), :, :].rearrange("a p n -> (a p) n")
                                 ).then_inc(unit_in[r], 16)
            tiles_used = sp.value_load(fmisc[0:1, 1, E - 1:E], min_val=E, max_val=TILES_MAX)
            sp.wait_ge(S["y_added"], 16 * tiles_used)
            sp.dma_start(out, acc[0:N, :]).then_inc(S["out_done"], 16)
            sp.wait_ge(S["out_done"], 16)

        @block.gpsimd
        def _(pool):
            pool.memset(edge_i[:, 1], FAR)
            pool.memset(edge_f[:, 1, :], 0.0).then_inc(S["pads_set"], 1)
            pool.memset(row2[:, :, DEST + 2:ROW], 0.0).then_inc(S["rowpad_done"], 1)
            pool.memset(mcum[:, 0, :], 0.0).then_inc(S["mcum_zero"], 1)

            def split_block(j):
                pool.wait_ge(S["win_merged"], 2 * j + 2)
                pool.tensor_copy(wT[:, 0, bass.ds(j, 1), :].rearrange("p a n -> p (a n)"), wsum).then_inc(S["wsplit_hi"], 1)
                pool.wait_ge(S["wsplit_hi"], j + 1)
                hi = wT[:, 0, bass.ds(j, 1), :].rearrange("p a n -> p (a n)")
                lo = wT[:, 1, bass.ds(j, 1), :].rearrange("p a n -> p (a n)")
                pool.tensor_tensor(lo, wsum, hi, ALU.subtract).then_inc(S["wsplit_done"], 1)

            def low1(t, h):
                pool.wait_ge(S["hi1_done"], t + 1)
                pool.tensor_tensor(row1[:, h, D:2 * D], xln[:], row1[:, h, 0:D], ALU.subtract
                                   ).then_inc(S["lo1_done"], 1)

            def bias_sum(t, h):
                pool.wait_ge(x_in[h], 16 * (t // 2 + 1))
                if known(t, 2):
                    pool.wait_ge(S["x1_done"], t - 1)
                pool.tensor_tensor(xb[:, h, :], xin[:, h, :], biasb[:], ALU.add).then_inc(S["xb_done"], 1)

            pool.wait_ge(S["bcast_in"], 16)
            bias_sum(0, 0)
            low1(0, 0)
            low1(1, 1)
            with pool.Fori(0, WINS // 2) as j:
                split_block(j)

            def scatter(t, h):
                pool.wait_ge(S["slot_done"], t + 1)
                pool.wait_ge(S["gate_done"], t + 1)
                pool.wait_ge(S["lo2_done"], t + 1)
                pool.sem_inc(S["pool_passed"], 1)
                for c in range(2):
                    pool.indirect_dma_start(
                        lists, bass.IndirectOffsetOnAxis(ap=slot_i[:, h, c:c + 1], axis=0), row2[:, h, :].bitcast(I32), None
                    ).then_inc(listed[h], 16)

            def gnn_tile(t, h):
                if below(t, TILES - 1):
                    bias_sum(t + 1, 1 - h)
                if below(t, TILES - 2):
                    low1(t + 2, h)
                if known(t, 2):
                    scatter(t - 2, h)
                if known(t, 2) and h == 1:
                    low_unit(t)
                if isinstance(t, int) and t == 1:
                    pool.wait_ge(S["gnn_done"], 1)
                    pool.memset(brow, 0.0).then_inc(S["brow_zero"], 1)
                pool.wait_ge(S["hi2_done"], t + 1)
                pool.tensor_tensor(row2[:, h, D:2 * D], xln2[:], row2[:, h, 0:D], ALU.subtract
                                   ).then_inc(S["lo2_done"], 1)

            def low_unit(t):
                pool.wait_ge(S["hi_done"], t - 1)
                u = t - 2
                hi = slots[:, 0, 0, bass.ds(u, 1), :].rearrange("p a n -> p (a n)")
                lo = slots[:, 0, 1, bass.ds(u, 1), :].rearrange("p a n -> p (a n)")
                st = staging[:, bass.ds(u % RING, 1), :].rearrange("p a n -> p (a n)")
                pool.tensor_tensor(st, st, scale_col.to_broadcast([P, D]), ALU.mult).then_inc(S["odd_scaled"], 1)
                pool.wait_ge(S["odd_scaled"], t // 2)
                pool.tensor_tensor(lo, st, hi, ALU.subtract).then_inc(S["lo_odd"], 1)

            tiles(gnn_tile, pool)
            pool.wait_ge(S["consts_in"], 48)
            pool.wait_ge(S["xln_done"], TILES)
            pool.wait_ge(S["lo2_done"], TILES)
            pool.memset(padrows, 0.0).then_inc(S["c_row"], 1)
            pool.wait_ge(S["c_row"], 1)
            pool.tensor_copy(padrows[:, DEST:DEST + 2].bitcast(I32), kdest[:, TILES:TILES + 1]).then_inc(S["padrow_done"], 1)
            scatter(TILES - 2, 0)
            scatter(TILES - 1, 1)

            pool.wait_ge(S["table_done"], 1)
            tiles_used = pool.value_load(fmisc[0:1, 1, E - 1:E], min_val=E, max_val=TILES_MAX)
            for h in range(2):
                pool.wait_ge(x1_out[h], 16 * (TILES // 2))
            with pool.Fori(0, tiles_used) as i:
                fresh = pool.value_load(ftab[0:1, 2, bass.ds(i, 1)], min_val=0, max_val=1)
                e = pool.value_load(ftab[0:1, 0, bass.ds(i, 1)], min_val=0, max_val=E - 1)
                with pool.If(fresh * (E - 1 - e) > 0):
                    for q in range(UNITS // 2):
                        pool.wait_ge(S["hi_done"], UNITS * (e + 1) + 2 * q + 2)
                        base = slots[:, bass.ds((e + 1) & 1, 1), :, 2 * q + 1, :].rearrange("p a s n -> p (a s) n")
                        st = staging[:, (2 * q + 1) % RING, :]
                        pool.tensor_tensor(st, st, scale_col.to_broadcast([P, D]), ALU.mult).then_inc(S["odd_scaled"], 1)
                        pool.wait_ge(S["odd_scaled"], 4 * e + 4 + q + 1)
                        pool.tensor_tensor(base[:, 1, :], st, base[:, 0, :], ALU.subtract).then_inc(S["lo_odd"], 1)
                pool.wait_ge(S["y_done"], i + 1)
                pool.wait_ge(S["dest_done"], i + 1)
                pool.sem_inc(S["pool_passed"], 1)
                pool.indirect_dma_start(acc, bass.IndirectOffsetOnAxis(ap=dest_i[:, 0:1], axis=0), yout, None,
                                        compute_op=ALU.add).then_inc(S["y_added"], 16)
                pool.wait_ge(S["y_added"], 16 * (i + 1))

        @block.scalar
        def _(act):
            def norm1(t, h):
                act.wait_ge(S["stats1_done"], t + 1)
                if known(t, 1):
                    act.wait_ge(S["lo1_done"], t)
                act.activation(xln[:], xin[:, h, :], ACT.Identity, bias=ab1[:, h, 1:2], scale=ab1[:, h, 0:1]
                               ).then_inc(S["xln_done"], 1)
                act.wait_ge(S["xln_done"], t + 1)
                if known(t, 2):
                    act.wait_ge(S["t1_done"], t - 1)
                act.copy(row1[:, h, 0:D], xln[:]).then_inc(S["hi1_done"], 1)

            norm1(0, 0)
            norm1(1, 1)
            act.wait_ge(S["parts_done"], 1)
            act.wait_ge(S["dst1h_done"], 1)
            act.wait_ge(S["wtab_done"], 1)

            def stat_group(g):
                for k in range(GRP):
                    c = g * GRP + k
                    one = dst1h[:, bass.ds(c, 1), :].rearrange("p a n -> p (a n)")
                    to = stat[:, bass.ds(c, 1), :].rearrange("p a n -> p (a n)")
                    act.activation(to[:, 0:WIN], one, ACT.Copy, scale=whl[:, 0, bass.ds(c, 1)])
                    ins = act.activation(to[:, WIN:2 * WIN], one, ACT.Copy, scale=whl[:, 1, bass.ds(c, 1)])
                    ins.then_inc(S["stat_done"], 1)

            def stats_for(w):
                begin = act.value_load(wtab[0:1, 3, bass.ds(w, 1)], min_val=0, max_val=NCH // GRP)
                end = act.value_load(wtab[0:1, 4, bass.ds(w, 1)], min_val=0, max_val=NCH // GRP)
                with act.If(end > begin):
                    with act.Fori(begin, end) as g:
                        stat_group(within(g, 0, NCH // GRP - 1))

            def bring_low(w, h):
                groups = act.value_load(wtab[0:1, 1, bass.ds(w, 1)], min_val=2, max_val=NCH // GRP)
                before = act.value_load(wtab[0:1, 2, bass.ds(w, 1)], min_val=0, max_val=WINS * NCH // GRP)
                act.wait_ge(src1h_used[GRP - 1], before + groups + 1)
                if not (isinstance(w, int) and w == 0):
                    act.wait_ge(S["win_merged"], w)
                act.copy(wlow, psW[WIN:2 * WIN, 2 * h:2 * h + 2, :].rearrange("p a n -> p (a n)")
                         ).then_inc(S["low_brought"], 1)

            stats_for(0)
            stats_for(1)
            stats_for(2)
            bring_low(0, 0)
            with act.Fori(1, WINS // 2 - 1) as i:
                stats_for(2 * i + 1)
                bring_low(2 * i - 1, 1)
                stats_for(2 * i + 2)
                bring_low(2 * i, 0)
            stats_for(WINS - 1)
            for w in range(WINS - 3, WINS):
                bring_low(w, w % 2)

            def gnn_tile(t, h):
                if known(t, 1):
                    act.wait_ge(S["nb_done"], t)
                    if known(t, 2):
                        act.wait_ge(S["gate_done"], t - 1)
                    act.activation(ex[:], m8[:, 1:2], ACT.Exp, bias=nb[:], scale=1.0 / SCALE).then_inc(S["exp_done"], 1)
                if below(t, TILES - 2):
                    norm1(t + 2, h)
                if known(t, 2):
                    high_unit(t - 2)
                act.wait_ge(S["stats2_done"], t + 1)
                if known(t, 1):
                    act.wait_ge(S["lo2_done"], t)
                act.activation(xln2[:], x1[:, h, :], ACT.Identity, bias=ab2[:, h, 1:2], scale=ab2[:, h, 0:1]
                               ).then_inc(S["xln2_done"], 1)
                act.wait_ge(S["xln2_done"], t + 1)
                if known(t, 2):
                    act.wait_ge(listed[h], 32 * (t // 2))
                act.copy(row2[:, h, 0:D], xln2[:]).then_inc(S["hi2_done"], 1)

            def high_unit(u):
                r = u % RING
                act.wait_ge(unit_in[r], 16 * (u // RING + 1))
                act.activation(slots[:, 0, 0, u, :], staging[:, r, :], ACT.Copy, scale=SCALE).then_inc(S["hi_done"], 1)

            for t in range(TILES):
                gnn_tile(t, t % 2)
            act.wait_ge(S["nb_done"], TILES)
            act.wait_ge(S["gate_done"], TILES - 1)
            act.activation(ex[:], m8[:, 1:2], ACT.Exp, bias=nb[:], scale=1.0 / SCALE).then_inc(S["exp_done"], 1)

            act.wait_ge(S["table_done"], 1)
            last = act.value_load(fmisc[0:1, 2, E - 1:E], min_val=E - 1, max_val=TILES_MAX - 1)
            for h in range(2):
                act.wait_ge(listed[h], 32 * (TILES // 2))
            act.wait_ge(S["pads_out"], 16 * E)
            act.wait_ge(S["brow_zero"], 1)

            def load_rows(i):
                row = act.value_load(ftab[0:1, 1, i:i + 1] if isinstance(i, int) else ftab[0:1, 1, bass.ds(i, 1)],
                                     min_val=0, max_val=DUMP - P)
                place = xs[:, i & 3, :] if isinstance(i, int) else xs[:, bass.ds(i & 3, 1), :].rearrange("p a n -> p (a n)")
                act.dma_start(place.bitcast(I32), lists[bass.ds(row, P), :]).then_inc(S["xs_in"], 16)

            def gelu(i):
                act.wait_ge(S["l1_done"], i + 1)
                act.activation(hgelu, psH, ACT.Gelu, scale=1.0 / SCALE).then_inc(S["gelu_done"], 1)
                act.wait_ge(S["gelu_done"], i + 1)
                act.copy(hsplit[:, 0, :], hgelu).then_inc(S["hhi_done"], 1)

            def gated(i):
                act.wait_ge(S["l2_done"], i + 1)
                act.wait_ge(S["gatec_done"], i + 1)
                if not (isinstance(i, int) and i == 0):
                    act.wait_ge(S["y_added"], 16 * i)
                act.activation(yout, psA[:].rearrange("p a n -> p (a n)"), ACT.Copy, scale=gate_f[:]
                               ).then_inc(S["y_done"], 1)

            def next_weights(i):
                fresh = act.value_load(ftab[0:1, 2, bass.ds(i, 1)], min_val=0, max_val=1)
                e = act.value_load(ftab[0:1, 0, bass.ds(i, 1)], min_val=0, max_val=E - 1)
                with act.If(fresh * (E - 1 - e) > 0):
                    for u in range(UNITS):
                        act.wait_ge(unit_in[u % RING], 32 * e + 16 * (u // RING) + 48)
                        to = slots[:, bass.ds((e + 1) & 1, 1), 0, u, :].rearrange("p a n -> p (a n)")
                        act.activation(to, staging[:, u % RING, :], ACT.Copy, scale=SCALE).then_inc(S["hi_done"], 1)

            load_rows(0)
            act.wait_ge(S["xs_in"], 16)
            load_rows(1)
            gelu(0)
            with act.Fori(0, last) as i:
                act.wait_ge(S["xs_in"], 16 * (i + 2))
                load_rows(i + 2)
                gelu(i + 1)
                next_weights(i)
                gated(i)
            gated(last)
            act.wait_ge(S["xs_in"], 16 * (last + 2))
            act.sem_inc(S["act_passed"], 1)

        @block.vector
        def _(dve):
            c_edge = Chain(dve, S["c_edge"], 10 ** 6)
            c_rng = Chain(dve, S["c_rng"], 10 ** 6)
            c_tab = Chain(dve, S["c_tab"], 10 ** 6)
            LN = 16
            c_ln1 = Chain(dve, S["c_ln1"], LN)
            c_ln2 = Chain(dve, S["c_ln2"], LN)
            c_rt = Chain(dve, S["c_rt"], 11)
            c_rk = Chain(dve, S["c_rk"], 4)

            def stats(chain, t, src_tile, st, mv, ab, done):
                chain.start(t)
                chain.inc(dve.bn_stats(st[:, 0, :], src_tile[:, 0:HALF]))
                chain.link_apart(dve.bn_stats(st[:, 1, :], src_tile[:, HALF:D]), S["dve_passed"])
                chain.link(dve.bn_aggr(mv[:, 0:2], st[:, :, :]))
                ve, y, q = mv[:, 2:3], mv[:, 3:4], mv[:, 4:5]
                chain.link(dve.tensor_scalar(ve, mv[:, 1:2], EPS, None, ALU.add))
                chain.link(dve.tensor_scalar(y.bitcast(I32), ve.bitcast(I32), 1, None, ALU.logical_shift_right))
                chain.link(dve.tensor_scalar(y.bitcast(I32), y.bitcast(I32), -1, MAGIC, ALU.mult, ALU.add))
                for n in range(3):
                    chain.link(dve.scalar_tensor_tensor(q, y, ve, y, ALU.mult, ALU.mult))
                    chain.link(dve.tensor_scalar(q, q, -0.5, 1.5, ALU.mult, ALU.add))
                    to = y if n < 2 else ab[:, 0:1]
                    chain.link(dve.tensor_tensor(to, y, q, ALU.mult))
                chain.link(dve.tensor_scalar(mv[:, 5:6], mv[:, 0:1], -1.0, None, ALU.mult))
                dve.tensor_tensor(ab[:, 1:2], mv[:, 5:6], ab[:, 0:1], ALU.mult).then_inc(done, 1)

            def stats1(t, h):
                dve.wait_ge(x_in[h], 16 * (t // 2 + 1))
                if known(t, 2):
                    dve.wait_ge(S["xln_done"], t - 1)
                stats(c_ln1, t, xin[:, h, :], st1, mv1, ab1[:, h, :], S["stats1_done"])

            L = c_edge.link
            dve.wait_ge(S["edges_in"], 16 * 9)
            dve.wait_ge(S["consts_in"], 16 * 3)
            c_edge.start(0)
            L(dve.tensor_scalar(tmp_i, edge_i[:, :, 1, :], 6, None, ALU.arith_shift_right))
            L(dve.tensor_copy(quant[:, :, 0, :], tmp_i))
            L(dve.tensor_scalar(tmp_i, edge_i[:, :, 1, :], WIN - 1, None, ALU.bitwise_and))
            c_edge.inc(dve.tensor_copy(quant[:, :, 1, :], tmp_i))
            c_edge.inc(dve.tensor_scalar(quant[:, :, 2, :], edge_i[:, :, 0, :], 1.0, None, ALU.add))
            L(dve.tensor_scalar(quant[:, :, 3, :], edge_f, SCALE, None, ALU.mult))
            dve.engine_nop().then_inc(S["quant_done"], 1)
            R = c_rng.link
            c_rng.start(0)
            c_rng.inc(dve.tensor_reduce(bmm[:, 0, :], quant[:, :, 0, :], AX.X, ALU.min))
            R(dve.tensor_reduce(bmm[:, 1, :], quant[:, :, 0, :], AX.X, ALU.max))
            wi = k32[:, S_I16:S_I16 + WINS]
            for h in range(2):
                R(dve.tensor_scalar(touch[:, h, 0, :], wi, bmm[:, 0, h:h + 1], None, ALU.is_ge))
                R(dve.scalar_tensor_tensor(touch[:, h, 1, :], wi, bmm[:, 1, h:h + 1], touch[:, h, 0, :], ALU.is_le, ALU.mult))
                R(dve.tensor_scalar(touch[:, h, 0, :], touch[:, h, 1, :], k32[:, S_CH + h:S_CH + h + 1], -BIG,
                                    ALU.mult, ALU.add))
                R(dve.tensor_scalar(touch[:, h, 1, :], touch[:, h, 1, :], k32[:, S_CH + 2 + h:S_CH + 3 + h], None, ALU.mult))
            R(dve.tensor_tensor(lohi[:].rearrange("p (a w) -> p a w", a=2), touch[:, 0], touch[:, 1], ALU.max))
            dve.engine_nop().then_inc(S["range_done"], 1)
            dve.wait_ge(S["edges_turned"], 1)
            L(dve.tensor_copy(eT[:], psA[:].rearrange("p a n -> p (a n)").rearrange("p (q n) -> p q n", q=4)))
            L(dve.tensor_copy(whi16[:], eT[:, 3, :]))
            L(dve.tensor_copy(whl[:, 0, :], whi16[:]))
            L(dve.tensor_tensor(whl[:, 1, :], eT[:, 3, :], whl[:, 0, :], ALU.subtract))
            dve.engine_nop().then_inc(S["parts_done"], 1)
            dve.tensor_tensor(dst1h, eT[:, 1, 0:NCH].unsqueeze(2).to_broadcast([P, NCH, WIN]),
                              k32[:, S_I64:S_I64 + WIN].unsqueeze(1).to_broadcast([P, NCH, WIN]),
                              ALU.is_equal).then_inc(S["dst1h_done"], 1)
            for w in range(WINS):
                c_edge.inc(dve.scalar_tensor_tensor(srcw[:, w, :], eT[:, 0, 0:NCH], float(w), eT[:, 2, 0:NCH],
                                                    ALU.is_equal, ALU.mult))
            dve.wait_ge(S["range_turned"], 1)
            R(dve.tensor_reduce(lohiT[:], psT[0:2 * WINS, 0].rearrange("p a n -> p (a n)").bitcast(F32)[:, 0:P], AX.X, ALU.max))
            dve.engine_nop().then_inc(S["range_row"], 1)
            dve.wait_ge(S["range_turned"], 2)
            R(dve.tensor_copy(wrow[:, 0:2, :].rearrange("p a w -> p (a w)"),
                              psT[0:1, 1].rearrange("p a n -> p (a n)").bitcast(F32)[:, 0:2 * WINS]))
            R(dve.scalar_tensor_tensor(wrow[:, 2, :], wrow[:, 0, :], -1.0, wrow[:, 1, :], ALU.mult, ALU.min))
            R(dve.tensor_scalar(wrow[:, 2, :], wrow[:, 2, :], float(NCH - 2 * GRP), None, ALU.min))
            R(dve.tensor_tensor(wrow[:, 3, :], wrow[:, 1, :], wrow[:, 2, :], ALU.subtract))
            R(dve.tensor_scalar(wrow[:, 3, :], wrow[:, 3, :], float(GRP - 1), None, ALU.add))
            R(dve.tensor_copy(wtab[:, 0:2, :], wrow[:, 2:4, :]))
            R(dve.tensor_scalar(wtab[:, 1, :], wtab[:, 1, :], 2, None, ALU.arith_shift_right))
            R(dve.tensor_scalar(wtab[:, 1, :], wtab[:, 1, :], 2.0, None, ALU.max))
            R(dve.tensor_copy(wrow[:, 3, :], wtab[:, 1, :]))
            R(dve.memset(wrow[:, 5, :], 1.0))
            R(dve.tensor_tensor_scan(wrow[:, 4, :], wrow[:, 5, :], wrow[:, 3, :], 0.0, ALU.mult, ALU.add))
            R(dve.tensor_tensor(wtab[:, 2, :], wrow[:, 4, :], wrow[:, 3, :], ALU.subtract))
            R(dve.scalar_tensor_tensor(wtab[:, 4, :], wtab[:, 1, :], float(GRP), wtab[:, 0, :], ALU.mult, ALU.add))
            R(dve.tensor_scalar(wtab[:, 4, :], wtab[:, 4, :], float(GRP - 1), None, ALU.add))
            R(dve.tensor_scalar(wtab[:, 4, :], wtab[:, 4, :], 2, None, ALU.arith_shift_right))
            R(dve.tensor_copy(wrow[:, 3, :], wtab[:, 4, :]))
            R(dve.tensor_tensor_scan(wrow[:, 4, :], wrow[:, 5, :], wrow[:, 3, :], 0.0, ALU.mult, ALU.max))
            R(dve.memset(wtab[:, 3, 0:1], 0))
            R(dve.tensor_copy(wtab[:, 4, :], wrow[:, 4, :]))
            R(dve.tensor_copy(wtab[:, 3, 1:WINS], wrow[:, 4, 0:WINS - 1]))
            dve.engine_nop().then_inc(S["wtab_done"], 1)
            stats1(0, 0)
            stats1(1, 1)

            def onehots(g, w, c):
                for k in range(GRP):
                    dve.wait_ge(src1h_used[k], g + 1)
                    dve.tensor_scalar(ring1h[:, k, :], iota1, srcw[:, bass.ds(w, 1), bass.ds(c + k, 1)].rearrange(
                        "p a n -> p (a n)"), None, ALU.is_equal).then_inc(src1h_ready[k], 1)

            def window(w):
                first = dve.value_load(wtab[0:1, 0, bass.ds(w, 1)], min_val=0, max_val=NCH - 2 * GRP)
                groups = dve.value_load(wtab[0:1, 1, bass.ds(w, 1)], min_val=2, max_val=NCH // GRP)
                before = dve.value_load(wtab[0:1, 2, bass.ds(w, 1)], min_val=0, max_val=WINS * NCH // GRP)
                with dve.Fori(0, groups) as j:
                    onehots(before + j, w, within(first + GRP * j, 0, NCH - GRP))

            def merge(w, h):
                dve.wait_ge(S["low_brought"], w + 1)
                if h == 0 and not (isinstance(w, int) and w == 0):
                    dve.wait_ge(S["wsplit_done"], w // 2)
                dve.tensor_tensor(wsum[WIN * h:WIN * h + WIN, :],
                                  psW[0:WIN, 2 * h:2 * h + 2, :].rearrange("p a n -> p (a n)"), wlow, ALU.add
                                  ).then_inc(S["win_merged"], 1)

            window(0)
            window(1)
            merge(0, 0)
            with dve.Fori(1, WINS // 2) as i:
                window(2 * i)
                merge(2 * i - 1, 1)
                window(2 * i + 1)
                merge(2 * i, 0)
            merge(WINS - 1, 1)
            dve.wait_ge(S["biases_in"], 48)
            c_tab.start(0)
            T_ = c_tab.link
            T_(dve.tensor_scalar(rws[:, :, 0:E], rw[:], SCALE, None, ALU.mult))
            T_(dve.scalar_tensor_tensor(rws[:, :, E:2 * E], rw[:], SCALE, rws[:, :, 0:E], ALU.mult, ALU.subtract))
            T_(dve.tensor_scalar(b12[:, 0, :], brow12[:], SCALE, None, ALU.mult))
            T_(dve.scalar_tensor_tensor(b12[:, 1, :], brow12[:], SCALE, b12[:, 0, :], ALU.mult, ALU.subtract))
            dve.engine_nop().then_inc(S["rws_done"], 1)
            dve.engine_nop().then_inc(S["b12_lo"], 1)

            def copy_t1(t, h):
                dve.wait_ge(S["t1_done"], t + 1)
                if known(t, 2):
                    dve.wait_ge(S["gnn_done"], t - 1)
                dve.tensor_copy(xT[:, h], psT[:]).then_inc(S["t1_copied"], 1)

            def rank_slots(t, h):
                dve.wait_ge(S["rank_done"], t + 1)
                if known(t, 2):
                    dve.wait_ge(listed[h], 32 * (t // 2))
                c_rk.start(t)
                c_rk.link(dve.tensor_tensor(pos[:, 0, :], psK[:, 0:E], k32[:, S_EB:S_EB + E], ALU.add))
                c_rk.inc(dve.tensor_tensor(pos[:, 1, :], pos[:, 0, :], pick[:, 0, :], ALU.mult))
                c_rk.link(dve.tensor_tensor(pos[:, 2, :], pos[:, 0, :], pick[:, 1, :], ALU.mult))
                c_rk.link(dve.tensor_reduce(slotf[:], pos[:, 1:3, :], AX.X, ALU.add))
                dve.tensor_tensor(slot_i[:, h, :], slotf[:], dump_cols(t), ALU.add).then_inc(S["slot_done"], 1)

            def dump_cols(t):
                return k32[:, bass.ds(2 * t + S_DUMP, 2)]

            def mask_col(t):
                return k32[:, bass.ds(t + S_MASK, 1)]

            def dest_col(t):
                return kdest[:, bass.ds(t, 1)]

            def copy_t2(t):
                dve.wait_ge(S["t2_done"], t + 1)
                dve.tensor_copy(x2T, psT[:]).then_inc(S["t2_copied"], 1)

            def route(t, h):
                dve.wait_ge(S["router_done"], t + 1)
                c_rt.start(t)
                K = c_rt.link
                K(dve.tensor_copy(logit[:, 0, :], psR[:, 0:E]))
                c_rt.link_apart(dve.tensor_tensor(logit[:, 1, :], logit[:, 0, :], psR[:, E:2 * E], ALU.add), S["dve_passed"])
                c_rt.link_apart(dve.max(m8[:], logit[:, 1, :]), S["dve_passed"])
                K(dve.max_index(i8[:], m8[:], logit[:, 1, :]))
                dve.tensor_scalar(nb[:], m8[:, 0:1], -1.0 / SCALE, None, ALU.mult).then_inc(S["nb_done"], 1)
                K(dve.tensor_copy(idf[:], i8[:, 0:2]))
                c_rt.inc(dve.tensor_scalar(pick[:, 0, :], k32[:, S_I8:S_I8 + E], idf[:, 0:1], mask_col(t), ALU.is_equal, ALU.mult))
                K(dve.tensor_scalar(pick[:, 1, :], k32[:, S_I8:S_I8 + E], idf[:, 1:2], mask_col(t), ALU.is_equal, ALU.mult))
                if known(t, 1):
                    dve.wait_ge(S["rank_done"], t)
                    dve.wait_ge(S["mask_done"], t)
                K(dve.tensor_tensor(mk[:, 0, :], pick[:, 0, :], pick[:, 1, :], ALU.add))
                dve.tensor_tensor(mcum[:, 1 - h, :], mcum[:, h, :], mk[:, 0, :], ALU.add).then_inc(S["mask_done"], 1)
                dve.wait_ge(S["exp_done"], t + 1)
                if known(t, 2):
                    dve.wait_ge(listed[h], 32 * (t // 2))
                K(dve.tensor_scalar(gs[:, 0:1], ex[:], 1.0, SCALE, ALU.add, ALU.mult))
                K(dve.reciprocal(gs[:, 1:2], gs[:, 0:1]))
                K(dve.tensor_tensor(gs[:, 2:3], ex[:], gs[:, 1:2], ALU.mult))
                dve.tensor_scalar(pick[:, 2, :], pick[:, 1, :], gs[:, 2:3], None, ALU.mult).then_inc(S["gates_built"], 1)
                dve.wait_ge(S["gates_built"], t + 1)
                dve.tensor_copy(row2[:, h, DEST:DEST + 2].bitcast(I32), dest_col(t)).then_inc(S["c_dest"], 1)
                dve.wait_ge(S["c_dest"], t + 1)
                dve.scalar_tensor_tensor(row2[:, h, GATE:DEST].bitcast(F32), pick[:, 0, :], gs[:, 1:2], pick[:, 2, :],
                                         ALU.mult, ALU.add).then_inc(S["gate_done"], 1)

            def low_unit(t):
                dve.wait_ge(S["hi_done"], t - 1)
                u = t - 2
                hi = slots[:, 0, 0, bass.ds(u, 1), :].rearrange("p a n -> p (a n)")
                lo = slots[:, 0, 1, bass.ds(u, 1), :].rearrange("p a n -> p (a n)")
                st = staging[:, bass.ds(u % RING, 1), :].rearrange("p a n -> p (a n)")
                dve.scalar_tensor_tensor(lo, st, SCALE, hi, ALU.mult, ALU.subtract).then_inc(S["lo_even"], 1)

            def gnn_tile(t, h):
                if below(t, TILES - 1):
                    copy_t1(t + 1, 1 - h)
                if known(t, 2):
                    rank_slots(t - 2, h)
                if known(t, 1):
                    copy_t2(t - 1)
                    route(t - 1, 1 - h)
                if below(t, TILES - 2):
                    stats1(t + 2, h)
                if known(t, 2) and h == 0:
                    low_unit(t)
                dve.wait_ge(S["gnn_done"], t + 1)
                dve.wait_ge(S["xb_done"], t + 1)
                if known(t, 2):
                    dve.wait_ge(x1_out[h], 16 * (t // 2))
                    dve.wait_ge(S["xln2_done"], t - 1)
                dve.scalar_tensor_tensor(x1[:, h, :], psA[:].rearrange("p a n -> p (a n)"), 1.0 / SCALE, xb[:, h, :],
                                         ALU.mult, ALU.add).then_inc(S["x1_done"], 1)
                dve.wait_ge(S["x1_done"], t + 1)
                stats(c_ln2, t, x1[:, h, :], st2, mv2, ab2[:, h, :], S["stats2_done"])

            dve.wait_ge(S["mcum_zero"], 1)
            copy_t1(0, 0)
            tiles(gnn_tile, dve)
            rank_slots(TILES - 2, 0)
            copy_t2(TILES - 1)
            route(TILES - 1, 1)
            rank_slots(TILES - 1, 1)

            dve.wait_ge(S["count_done"], 1)
            T_(dve.tensor_copy(cnts[:, 0, :], psK[0:1, E:2 * E]))
            T_(dve.tensor_scalar(cnts[:, 1, :], cnts[:, 0, :], float(P - 1), None, ALU.add))
            T_(dve.tensor_copy(cnti[:, 0, :], cnts[:, 1, :]))
            T_(dve.tensor_scalar(cnti[:, 0, :], cnti[:, 0, :], 7, None, ALU.arith_shift_right))
            T_(dve.tensor_scalar(cnts[:, 2, :], cnti[:, 0, :], 1.0, None, ALU.max))
            T_(dve.memset(cnts[:, 3, :], 1.0))
            T_(dve.tensor_tensor_scan(cnts[:, 4, :], cnts[:, 3, :], cnts[:, 2, :], 0.0, ALU.mult, ALU.add))
            T_(dve.tensor_copy(fmisc[:, 1, :], cnts[:, 4, :]))
            T_(dve.tensor_scalar(fmisc[:, 2, :], cnts[:, 4, :], -1.0, None, ALU.add))
            T_(dve.tensor_tensor(fmisc[:, 0, :], cnts[:, 0, :], k32[0:1, S_EB:S_EB + E], ALU.add))
            ti = k32[0:1, S_IT:S_IT + TMAX]
            T_(dve.tensor_tensor(tt[:, 0], ti.unsqueeze(2).to_broadcast([1, TMAX, E]),
                                 cnts[:, 4, :].unsqueeze(1).to_broadcast([1, TMAX, E]), ALU.is_ge))
            T_(dve.tensor_tensor(tt[:, 1], tt[:, 0], cnts[:, 2, :].unsqueeze(1).to_broadcast([1, TMAX, E]), ALU.mult))
            T_(dve.tensor_reduce(tf[:, 0, :], tt[:, 0], AX.X, ALU.add))
            T_(dve.tensor_reduce(tf[:, 1, :], tt[:, 1], AX.X, ALU.add))
            T_(dve.tensor_scalar(tf[:, 2, :], tf[:, 0, :], float(E - 1), None, ALU.min))
            T_(dve.tensor_copy(ftab[:, 0, :], tf[:, 2, :]))
            T_(dve.tensor_tensor(tf[:, 3, :], ti, tf[:, 1, :], ALU.subtract))
            T_(dve.tensor_scalar(ftab[:, 2, :], tf[:, 3, :], 0.0, None, ALU.is_equal))
            T_(dve.tensor_scalar(tf[:, 4, :], tf[:, 3, :], float(P), None, ALU.mult))
            T_(dve.scalar_tensor_tensor(ftab[:, 1, :], tf[:, 2, :], float(CAP), tf[:, 4, :], ALU.mult, ALU.add))
            dve.engine_nop().then_inc(S["table_done"], 1)

            last = dve.value_load(fmisc[0:1, 2, E - 1:E], min_val=E - 1, max_val=TILES_MAX - 1)

            def copy_rows(i):
                dve.wait_ge(S["xs_done"], i + 1)
                dve.tensor_copy(xsT, psT[:]).then_inc(S["xsT_copied"], 1)

            def split_h(i):
                dve.wait_ge(S["hhi_done"], i + 1)
                dve.tensor_tensor(hsplit[:, 1, :], hgelu, hsplit[:, 0, :], ALU.subtract).then_inc(S["hlo_done"], 1)

            def copy_h(i):
                dve.wait_ge(S["ht_done"], i + 1)
                dve.tensor_copy(hT[:, :, 0:FB, :], psHT).then_inc(S["ht_copied"], 1)

            def targets(i, e):
                if not (isinstance(i, int) and i == 0):
                    dve.wait_ge(S["y_done"], i)
                    dve.wait_ge(S["y_added"], 16 * i)
                dve.wait_ge(S["xs_in"], 16 * (i + 1))
                place = xs[:, bass.ds(i & 3, 1), :].rearrange("p a n -> p (a n)")
                dve.tensor_copy(gate_f[:], place[:, GATE:DEST].bitcast(F32)[:, bass.ds(e, 1)]).then_inc(S["gatec_done"], 1)
                dve.tensor_copy(dest_i[:], place[:, DEST:DEST + 2].bitcast(I32)).then_inc(S["dest_done"], 1)

            copy_rows(0)
            split_h(0)
            copy_rows(1)
            copy_h(0)
            with dve.Fori(0, last) as i:
                fresh = dve.value_load(ftab[0:1, 2, bass.ds(i, 1)], min_val=0, max_val=1)
                e = dve.value_load(ftab[0:1, 0, bass.ds(i, 1)], min_val=0, max_val=E - 1)
                split_h(i + 1)
                targets(i, e)
                copy_rows(i + 2)
                with dve.If(fresh * (E - 1 - e) > 0):
                    for q in range(UNITS // 2):
                        dve.wait_ge(S["hi_done"], UNITS * (e + 1) + 2 * q + 1)
                        base = slots[:, bass.ds((e + 1) & 1, 1), :, 2 * q, :].rearrange("p a s n -> p (a s) n")
                        dve.scalar_tensor_tensor(base[:, 1, :], staging[:, 2 * q % RING, :], SCALE, base[:, 0, :],
                                                 ALU.mult, ALU.subtract).then_inc(S["lo_even"], 1)
                copy_h(i + 1)
            targets(last, E - 1)

        @block.tensor
        def _(pe):
            pe.wait_ge(S["quant_done"], 1)
            turned = psA[:].rearrange("p a n -> p (a n)").rearrange("p (q h n) -> p q h n", q=4, h=2)
            for q in range(4):
                for h in range(2):
                    ins = pe.transpose(turned[:, q, h, :], quant[:, h, q, :], ident32)
            ins.then_inc(S["edges_turned"], 1)
            pe.wait_ge(S["range_done"], 1)
            pe.transpose(psT[0:2 * WINS, 0].rearrange("p a n -> p (a n)").bitcast(F32)[:, 0:P], lohi[:], ident32
                         ).then_inc(S["range_turned"], 1)
            pe.wait_ge(S["range_row"], 1)
            pe.transpose(psT[0:1, 1].rearrange("p a n -> p (a n)").bitcast(F32)[:, 0:2 * WINS], lohiT[:],
                         ident32[0:2 * WINS, 0:2 * WINS]).then_inc(S["range_turned"], 1)
            for k in range(GRP):
                pe.sem_inc(src1h_used[k], 1)
            pe.wait_ge(S["wtab_done"], 1)

            def group(g, c, h, start):
                for k in range(GRP):
                    pe.wait_ge(S["stat_done"], c + k + 1)
                    pe.wait_ge(src1h_ready[k], g + 1)
                    st = stat[:, bass.ds(c + k, 1), :].rearrange("p a n -> p (a n)")
                    for b in range(2):
                        ins = pe.matmul(psW[:, 2 * h + b, :], st, ring1h[:, k, b * HALF:(b + 1) * HALF],
                                        start=(start and k == 0), stop=False, skip_group_check=True)
                    ins.then_inc(src1h_used[k], 1)

            def window(w, h):
                first = pe.value_load(wtab[0:1, 0, bass.ds(w, 1)], min_val=0, max_val=NCH - 2 * GRP)
                groups = pe.value_load(wtab[0:1, 1, bass.ds(w, 1)], min_val=2, max_val=NCH // GRP)
                before = pe.value_load(wtab[0:1, 2, bass.ds(w, 1)], min_val=0, max_val=WINS * NCH // GRP)
                if not isinstance(w, int):
                    pe.wait_ge(S["win_merged"], w - 1)
                group(before, first, h, True)
                with pe.Fori(1, groups) as j:
                    group(before + j, within(first + GRP * j, 0, NCH - GRP), h, False)

            window(0, 0)
            window(1, 1)
            with pe.Fori(1, WINS // 2) as i:
                window(2 * i, 0)
                window(2 * i + 1, 1)

            def turn(rows, out_t, done):
                for part in range(2):
                    for k in range(KB):
                        ins = pe.transpose(out_t[:, part, k, :], rows[:, part * D + k * P:part * D + (k + 1) * P], ident)
                ins.then_inc(done, 1)

            def turn1(t, h):
                pe.wait_ge(S["lo1_done"], t + 1)
                if known(t, 1):
                    pe.wait_ge(S["t1_copied"], t)
                if known(t, 3):
                    pe.wait_ge(S["t2_copied"], t - 2)
                turn(row1[:, h, :], psT, S["t1_done"])

            def rank(t, h):
                pe.wait_ge(S["mask_done"], t + 1)
                if known(t, 1):
                    pe.wait_ge(S["slot_done"], t)
                pe.matmul(psK[:, 0:E], tri, mk[:, 0, :], start=True, stop=False)
                pe.matmul(psK[:, 0:E], ones, mcum[:, h, :], start=False, stop=True).then_inc(S["rank_done"], 1)

            def turn2(t, h):
                pe.wait_ge(S["lo2_done"], t + 1)
                pe.wait_ge(S["t1_copied"], t + 3 if below(t, TILES - 2) and not isinstance(t, int) else min(t + 3, TILES))
                if known(t, 1):
                    pe.wait_ge(S["t2_copied"], t)
                turn(row2[:, h, :], psT, S["t2_done"])

            def router_mm(t):
                pe.wait_ge(S["t2_copied"], t + 1)
                if known(t, 1):
                    pe.wait_ge(S["mask_done"], t)
                for part in range(2):
                    for k in range(KB):
                        ins = pe.matmul(psR[:, 0:2 * E], x2T[:, part, k, :], rws[:, k, :],
                                        start=(part == 0 and k == 0), stop=(part == 1 and k == KB - 1))
                ins.then_inc(S["router_done"], 1)

            def gnn_tile(t, h):
                if below(t, TILES - 1):
                    turn1(t + 1, 1 - h)
                if known(t, 2):
                    rank(t - 2, h)
                pe.wait_ge(S["t1_copied"], t + 1)
                if known(t, 1):
                    pe.wait_ge(S["x1_done"], t)
                for k in range(KB):
                    for part, wpart in ((0, 0), (0, 1), (1, 0)):
                        for b in range(2):
                            ins = pe.matmul(psA[:, b, :], xT[:, h, part, k, :], wT[:, wpart, k, b * HALF:(b + 1) * HALF],
                                            start=(k == 0 and part == 0 and wpart == 0), stop=(k == KB - 1 and part == 1))
                ins.then_inc(S["gnn_done"], 1)
                if known(t, 1):
                    turn2(t - 1, 1 - h)
                    router_mm(t - 1)

            pe.wait_ge(S["wsplit_done"], WINS // 2)
            pe.wait_ge(S["rws_done"], 1)
            turn1(0, 0)
            tiles(gnn_tile, pe)
            rank(TILES - 2, 0)
            turn2(TILES - 1, 1)
            router_mm(TILES - 1)
            rank(TILES - 1, 1)
            pe.wait_ge(S["slot_done"], TILES)
            pe.matmul(psK[:, E:2 * E], ones, mcum[:, 0, :], start=True, stop=True).then_inc(S["count_done"], 1)

            pe.wait_ge(S["table_done"], 1)
            pe.wait_ge(S["brow_in"], 32)
            last = pe.value_load(fmisc[0:1, 2, E - 1:E], min_val=E - 1, max_val=TILES_MAX - 1)

            def turn_rows(i):
                pe.wait_ge(S["xs_in"], 16 * (i + 1))
                if not (isinstance(i, int) and i == 0):
                    pe.wait_ge(S["xsT_copied"], i)
                place = xs[:, i & 3, :] if isinstance(i, int) else xs[:, bass.ds(i & 3, 1), :].rearrange("p a n -> p (a n)")
                turn(place, psT, S["xs_done"])

            def layer1(i, e):
                pe.wait_ge(S["xsT_copied"], i + 1)
                if not (isinstance(i, int) and i == 0):
                    pe.wait_ge(S["gelu_done"], i)
                pe.wait_ge(S["lo_even"], 4 * e + 4)
                pe.wait_ge(S["lo_odd"], 4 * e + 4)
                slot = slots[:, bass.ds(e & 1, 1)].rearrange("p o a b n -> p (o a) b n")
                pe.matmul(psH, ones2, brow[:, bass.ds(e * F, F)], start=True, stop=False)
                for k in range(KB):
                    cols = slice((k % 2) * F, (k % 2) * F + F)
                    for part, wpart in ((0, 0), (0, 1), (1, 0)):
                        ins = pe.matmul(psH, xsT[:, part, k, :], slot[:, wpart, k // 2, cols],
                                        start=False, stop=(k == KB - 1 and part == 1))
                ins.then_inc(S["l1_done"], 1)

            def turn_h(i):
                pe.wait_ge(S["hlo_done"], i + 1)
                if not (isinstance(i, int) and i == 0):
                    pe.wait_ge(S["ht_copied"], i)
                for part in range(2):
                    for f in range(FB):
                        ins = pe.transpose(psHT[:, part, f, :], hsplit[:, part, f * P:(f + 1) * P], ident)
                ins.then_inc(S["ht_done"], 1)

            def layer2(i, e):
                pe.wait_ge(S["ht_copied"], i + 1)
                if not (isinstance(i, int) and i == 0):
                    pe.wait_ge(S["y_done"], i)
                slot = slots[:, bass.ds(e & 1, 1)].rearrange("p o a b n -> p (o a) b n")
                for b in range(2):
                    pe.matmul(psA[:, b, :], ones2, brow[:, bass.ds(E * F + e * D + b * HALF, HALF)], start=True, stop=False)
                for f in range(FB):
                    for part, wpart in ((0, 0), (0, 1), (1, 0)):
                        for b in range(2):
                            ins = pe.matmul(psA[:, b, :], hT[:, part, f, :], slot[:, wpart, 4 + f, b * HALF:(b + 1) * HALF],
                                            start=False, stop=(f == FB - 1 and part == 1))
                ins.then_inc(S["l2_done"], 1)

            turn_rows(0)
            layer1(0, 0)
            turn_rows(1)
            turn_h(0)
            with pe.Fori(0, last) as i:
                e0 = pe.value_load(ftab[0:1, 0, bass.ds(i, 1)], min_val=0, max_val=E - 1)
                e1 = pe.value_load(ftab[0:1, 0, bass.ds(i + 1, 1)], min_val=0, max_val=E - 1)
                layer1(i + 1, e1)
                turn_rows(i + 2)
                layer2(i, e0)
                turn_h(i + 1)
            layer2(last, E - 1)


def constants(np):
    p = np.arange(P)
    k16 = np.zeros((P, H_END), np.float16)
    k16[:, H_ID:H_ID + P] = np.eye(P)
    k16[:, H_TRI:H_TRI + P] = p[:, None] < p[None, :]
    k16[:, H_ONE:H_ONE + P] = 1
    k16[0, H_ONE2:H_ONE2 + P] = 1
    k16[32, H_ONE2:H_ONE2 + P] = 1
    k16[:, H_IOTA:H_IOTA + D] = np.arange(1, D + 1)
    k32 = np.zeros((P, S_END), np.float32)
    k32[:, S_ID:S_ID + P] = np.eye(P)
    k32[:, S_I64:S_I64 + WIN] = np.arange(WIN)
    k32[:, S_I16:S_I16 + WINS] = np.arange(WINS)
    k32[:, S_I8:S_I8 + E] = np.arange(E)
    for h in range(2):
        k32[:, S_CH + h] = BIG - (p + P * h)
        k32[:, S_CH + 2 + h] = p + P * h + 1
    k32[:, S_EB:S_EB + E] = np.arange(E) * CAP
    k32[:, S_MASK:S_MASK + TILES] = 1
    k32[:REPEAT, S_MASK + TILES - 1] = 0
    for c in range(2):
        k32[:REPEAT, S_DUMP + 2 * (TILES - 1) + c] = DUMP + P * c + p[:REPEAT]
    k32[:, S_IT:S_IT + TMAX] = np.arange(TMAX)
    k32[:, S_SC] = SCALE
    kd = np.zeros((P, 16), np.int32)
    for t in range(TILES):
        kd[:, t] = min(P * t, LAST) + p
    kd[:, TILES] = N + p
    return k16, k32, kd


def kernel(x, src, dst, edge_weight, L0_gnn_bias, L0_ffn_router_w, L0_ffn_w1, L0_ffn_b1, L0_ffn_w2, L0_ffn_b2):
    import numpy as np
    import concourse.bacc as bacc
    from concourse.bass_utils import run_bass_kernel_spmd

    def lay(a):
        return np.ascontiguousarray(a)

    k16, k32, kd = constants(np)
    w1 = np.asarray(L0_ffn_w1).transpose(0, 2, 1).reshape(E, UNITS // 2, 2, P, F).transpose(0, 1, 3, 2, 4)
    w2 = np.asarray(L0_ffn_w2).transpose(0, 2, 1)
    arrays = {
        "x": lay(x), "src": lay(src), "dst": lay(dst), "edge_w": lay(edge_weight),
        "bias": lay(np.asarray(L0_gnn_bias).reshape(1, D)),
        "router": lay(np.asarray(L0_ffn_router_w).reshape(E, KB, P).transpose(2, 1, 0)),
        "w1u": lay(w1.reshape(E * UNITS // 2, P, 2 * F)), "w2u": lay(w2.reshape(E * FB, P, D)),
        "b1": lay(np.asarray(L0_ffn_b1).reshape(E * F // D, D)), "b2": lay(L0_ffn_b2),
        "c16": k16, "c32": k32, "ci": kd,
    }
    nc = bacc.Bacc("TRN2", target_bir_lowering=False, num_devices=1)
    args = {name: nc.dram_tensor(name, a.shape, mybir.dt.from_np(a.dtype), kind="ExternalInput").ap()
            for name, a in arrays.items()}
    out = nc.dram_tensor("out", (N, D), F32, kind="ExternalOutput").ap()
    build_program(nc, out=out, **args)
    r = run_bass_kernel_spmd(nc, [arrays], core_ids=[0])
    return r.results[0]["out"]
```

```python
from contextlib import ExitStack

import concourse.bass as bass
from concourse import mybir

ALU = mybir.AluOpType
ACT = mybir.ActivationFunctionType
AX = mybir.AxisListType
F32 = mybir.dt.float32
F16 = mybir.dt.float16
I32 = mybir.dt.int32
U32 = mybir.dt.uint32

P = 128
N = 1250
D = 1024
KB = D // P
NE = 21250
E = 8
F = 512
FB = F // P
HALF = 512
EPS = 1e-5
SCALE = 64.0
TILES = (N + P - 1) // P
LAST = N - P
REPEAT = P * TILES - N

WIN = 64
WINS = D // WIN
GRP = 4
CHUNKS = (NE + P - 1) // P
NCH = 172
FAR = 2 ** 20
BIG = 512.0

CAP = N // P * P + 2 * P
DUMP = E * CAP
TILES_MAX = (2 * N + E * (P - 1)) // P
TMAX = 32
UNITS = 8
RING = UNITS // 2
MAGIC = 0x5F3759DF

H_ID, H_TRI, H_ONE, H_ONE2, H_IOTA, H_END = 0, 128, 256, 384, 512, 512 + D
S_ID, S_I64, S_I16, S_I8, S_CH, S_EB, S_MASK, S_DUMP, S_IT, S_SC, S_END = (
    0, 128, 192, 208, 216, 220, 228, 238, 258, 290, 291)


class Chain:

    def __init__(self, eng, sem, per):
        self.eng, self.sem, self.per, self.base, self.n = eng, sem, per, 0, 0

    def start(self, index):
        assert self.n in (0, self.per), (self.n, self.per)
        self.base, self.n = index * self.per, 0

    def inc(self, ins):
        self.n += 1
        ins.then_inc(self.sem, 1)

    def link(self, ins):
        self.inc(ins)
        self.eng.wait_ge(self.sem, self.base + self.n)

    def link_apart(self, ins, passed):
        self.link(ins)
        self.eng.sem_inc(passed, 1)


def build_program(nc, x, src, dst, edge_w, bias, router, w1u, w2u, b1, b2, c16, c32, ci, cl, out):
    ctx = ExitStack()
    with ctx:
        def sb(name, shape, dt):
            return ctx.enter_context(nc.sbuf_tensor(name, shape, dt))

        def sem(name):
            return ctx.enter_context(nc.semaphore(name))

        lists = nc.dram_tensor("lists", [DUMP + 4 * P, 4], I32).ap()
        rows = nc.dram_tensor("rows", [N, D], I32).ap()
        acc = nc.dram_tensor("acc", [N + P, D], F32).ap()

        k16 = sb("k16", [P, H_END], F16)
        k32 = sb("k32", [P, S_END], F32)
        kdest = sb("kdest", [P, 4 * TILES], I32)
        slots = sb("slots", [P, 2, 2, UNITS, D], F16)
        wT = slots[:, 1]
        dst1h = slots[:, 0].rearrange("p a b c -> p (a b c)")[:, 0:NCH * WIN].rearrange("p (c n) -> p c n", n=WIN)
        late = sb("late", [P, NCH * 2 * WIN], F16)
        stat = late[:].rearrange("p (c n) -> p c n", n=2 * WIN)
        BCOLS = E * (F + D)
        brow = late[:, 0:BCOLS]
        xs = late[:, BCOLS:BCOLS + 2 * D]
        staging = sb("staging", [P, UNITS, D], F32)
        rows16 = staging[:, RING:UNITS, :].rearrange("p r n -> p (r n)").bitcast(F16).rearrange(
            "p (a h n) -> p a h n", a=2, h=2)
        ring1h = sb("ring1h", [P, GRP, D], F16)
        x1 = ring1h[:].rearrange("p r n -> p (r n)").bitcast(F32)[:, 0:2 * D].rearrange("p (r n) -> p r n", n=D)
        xin = sb("xin", [P, 2, D], F32)
        xb = sb("xb", [P, 2, D], F32)
        yout = xb[:, 0]
        hgelu = xb[:, 1, 0:F]
        hsplit = xb[:, 1].bitcast(F16)[:, 2 * F:4 * F].rearrange("p (s n) -> p s n", s=2)
        biasb = sb("biasb", [P, D], F32)
        xln = sb("xln", [P, D], F32)
        xln2 = sb("xln2", [P, D], F32)
        wsum = xln2[:]
        row1 = rows16[:, 0]
        row2 = rows16[:, 1]
        xTs = sb("xTs", [P, 3, 2, KB, P], F16)
        xT = xTs[:, 0:2]
        x2T = xTs[:, 2]
        srcw = xTs[:].rearrange("p a b c d -> p (a b c d)").bitcast(F32)[:, 0:WINS * NCH].rearrange(
            "p (w c) -> p w c", w=WINS)
        xsT = x2T
        hT = xTs[:, 0]
        edge_i = xln2[:, 0:4 * P].bitcast(I32).rearrange("p (h j e) -> p h j e", h=2, j=2)
        edge_f = xln2[:, 4 * P:6 * P].rearrange("p (h e) -> p h e", h=2)
        tmp_i = xln2[:, 6 * P:8 * P].bitcast(I32).rearrange("p (h e) -> p h e", h=2)
        quant = sb("quant", [P, 2, 4, P], F32)
        eT = sb("eT", [P, 4, 2 * P], F32)
        whi16 = sb("whi16", [P, 2 * P], F16)
        whl = sb("whl", [P, 2, 2 * P], F32)
        bmm = sb("bmm", [P, 2, 2], F32)
        touch = sb("touch", [P, 2, 2, WINS], F32)
        lohi = sb("lohi", [P, 2 * WINS], F32)
        lohiT = sb("lohiT", [2 * WINS, 1], F32)
        wrow = sb("wrow", [1, 6, WINS], F32)
        wtab = sb("wtab", [1, 5, WINS], I32)
        wlow = row2[0:WIN, 1, :].bitcast(F32)
        brow12 = row2[0:12, 0, :].bitcast(F32)
        b12 = eT[0:12].rearrange("p q n -> p (q n)").bitcast(F16).rearrange("p (a n) -> p a n", a=2)
        rw = sb("rw", [P, KB, E], F32)
        rws = sb("rws", [P, KB, 2 * E], F16)
        bn6 = sb("bn6", [P, 2, 2, 6], F32)
        mv = sb("mv", [P, 2, 2], F32)
        nwt = sb("nwt", [P, 5, 2], F32)
        ab0 = sb("ab0", [P, 2, 2], F32)
        ab = sb("ab", [P, 2, 2, 2], F32)
        logit = sb("logit", [P, 2, E], F32)
        m8 = sb("m8", [P, 8], F32)
        i8 = sb("i8", [P, 8], U32)
        idf = sb("idf", [P, 2], F32)
        nb = sb("nb", [P, 1], F32)
        ex = sb("ex", [P, 1], F32)
        gs = sb("gs", [P, 1], F32)
        ent = sb("ent", [P, 2, 2, 4], I32)
        pick = sb("pick", [P, 2, E], F32)
        mk = sb("mk", [P, 2, E], F16)
        mcum = sb("mcum", [P, 2, E], F16)
        pos = sb("pos", [P, 3, E], F32)
        slotf = sb("slotf", [P, 2], F32)
        slot_i = sb("slot_i", [P, 2, 2], I32)
        cnts = sb("cnts", [1, 6, E], F32)
        cnti = sb("cnti", [1, 4, E], I32)
        tt = quant[0:1].rearrange("p h q n -> p (h q n)")[:, 0:2 * TMAX * E].rearrange("p (a i e) -> p a i e", a=2, e=E)
        tf = sb("tf", [1, 6, TMAX], F32)
        ftab = sb("ftab", [1, 3, TMAX], I32)
        fmisc = sb("fmisc", [1, 3, E], I32)
        ents = sb("ents", [P, 8, 4], I32)
        gidx = sb("gidx", [P, 1], I32)
        dest_i = sb("dest_i", [P, 1], I32)

        psA = ctx.enter_context(nc.psum_tensor("psA", [P, 2, HALF], F32))
        psT = ctx.enter_context(nc.psum_tensor("psT", [P, 2, KB, P], F16))
        psW = ctx.enter_context(nc.psum_tensor("psW", [P, 4, HALF], F32))
        psG = (psA[:].rearrange("p a n -> p (a n)"), psW[:, 2:4, :].rearrange("p a n -> p (a n)"))
        psR = psW[:, 0]
        psK = psW[:, 1]
        psH = psW[:, 2]
        psHT = psW[:, 3].bitcast(F16).rearrange("p (s f n) -> p s f n", s=2, f=FB)

        s = {}
        for name in """consts_in edges_in biases_in brow_in bcast_in pads_set brow_zero quant_done edges_turned
                       parts_done dst1h_done wtab_done range_turned range_done range_row stat_done group_done
                       win_merged dve_passed pool_passed act_passed low_brought wsplit_done xln_done hi1_done lo1_done xb_done t1_done t1_copied
                       gnn_done x1_done stats_done xln2_done hi2_done lo2_done t2_done t2_copied router_done
                       nb_done exp_done gate_done mask_done rank_done slot_done count_done table_done rws_done
                       lists_set b12_lo mcum_zero wsplit_hi gidx_done
                       lo_done hi_done ents_in xs_in xs_done l1_done gelu_done hhi_done hlo_done ht_done ht_copied l2_done
                       y_done dest_done y_added out_done
                       xsT_copied c_edge c_rng c_ln c_rt c_rk c_tab c_row""".split():
            s[name] = sem(name)
        S = s
        src1h_ready = [sem(f"src1h_ready{g}") for g in range(GRP)]
        src1h_used = [sem(f"src1h_used{g}") for g in range(GRP)]
        x_in = [sem(f"x_in{h}") for h in range(2)]
        x1_out = [sem(f"x1_out{h}") for h in range(2)]
        row_out = [sem(f"row_out{h}") for h in range(2)]
        listed = [sem(f"listed{h}") for h in range(2)]
        unit_in = [sem(f"unit_in{r}") for r in range(UNITS)]

        ident = k16[:, H_ID:H_ID + P]
        tri = k16[:, H_TRI:H_TRI + P]
        ones = k16[:, H_ONE:H_ONE + P]
        ones2 = k16[:, H_ONE2:H_ONE2 + P]
        iota1 = k16[:, H_IOTA:H_IOTA + D]
        scale_col = k32[:, S_SC:S_SC + 1]
        ident32 = k32[:, S_ID:S_ID + P]

        def tile_start(t):
            return P * t - REPEAT * (t // (TILES - 1))

        def tiles(body, eng):
            body(0, 0)
            body(1, 1)
            with eng.Fori(1, TILES // 2 - 1) as i:
                body(2 * i, 0)
                body(2 * i + 1, 1)
            for t in range(TILES - 2, TILES + 2):
                body(t, t % 2)

        def within(v, low, high):
            return v if isinstance(v, int) else v.with_bounds(min_val=low, max_val=high)

        def known(t, low):
            return t >= low if isinstance(t, int) else True

        def below(t, high):
            return t < high if isinstance(t, int) else True

        block = ctx.enter_context(nc.Block())

        @block.sync
        def _(sp):
            full = NE // P - P
            rest = NE - (P + full) * P
            sp.dma_start(k32[:], c32).then_inc(S["consts_in"], 16)
            for j, a in enumerate((src, dst)):
                sp.dma_start(edge_i[:, 0, j, :], a[0:P * P].rearrange("(c e) -> c e", e=P)).then_inc(S["edges_in"], 16)
            sp.dma_start(edge_f[:, 0, :], edge_w[0:P * P].rearrange("(c e) -> c e", e=P)).then_inc(S["edges_in"], 16)
            sp.wait_ge(S["pads_set"], 1)
            for j, a in enumerate((src, dst)):
                sp.dma_start(edge_i[0:full, 1, j, :],
                             a[P * P:(P + full) * P].rearrange("(c e) -> c e", e=P)).then_inc(S["edges_in"], 16)
                sp.dma_start(edge_i[full:full + 1, 1, j, 0:rest],
                             a[(P + full) * P:NE].rearrange("(c e) -> c e", c=1)).then_inc(S["edges_in"], 16)
            sp.dma_start(edge_f[0:full, 1, :],
                         edge_w[P * P:(P + full) * P].rearrange("(c e) -> c e", e=P)).then_inc(S["edges_in"], 16)
            sp.dma_start(edge_f[full:full + 1, 1, 0:rest],
                         edge_w[(P + full) * P:NE].rearrange("(c e) -> c e", c=1)).then_inc(S["edges_in"], 16)
            sp.dma_start(k16[:], c16).then_inc(S["consts_in"], 16)
            sp.dma_start(kdest[:], ci).then_inc(S["consts_in"], 16)
            for h in range(2):
                sp.dma_start(xin[:, h, :], x[h * P:(h + 1) * P, :]).then_inc(x_in[h], 16)
            sp.dma_start(biasb[:], bias.to_broadcast([P, D])).then_inc(S["bcast_in"], 16)
            sp.dma_start(rw[:], router).then_inc(S["biases_in"], 16)
            sp.dma_start(brow12[0:4, :], b1).then_inc(S["biases_in"], 16)
            sp.dma_start(brow12[4:12, :], b2).then_inc(S["biases_in"], 16)
            for r in range(RING):
                sp.dma_start(staging[:, r, :], w1u[r, :, :]).then_inc(unit_in[r], 16)
            sp.dma_start(lists, cl).then_inc(S["lists_set"], 16)

            def load_x(t):
                sp.wait_ge(S["xb_done"], t - 1)
                sp.wait_ge(S["xln_done"], t - 1)
                sp.dma_start(xin[:, t % 2, :], x[bass.ds(tile_start(t), P), :]).then_inc(x_in[t % 2], 16)

            load_x(2)
            for t in range(TILES + 1):
                if 4 <= t < 4 + RING:
                    r = t - 4
                    sp.wait_ge(S["lo_done"], r + 1)
                    sp.dma_start(staging[:, r, :], w2u[r, :, :]).then_inc(unit_in[r], 16)
                u = t - 1
                if u == TILES - 1:
                    sp.wait_ge(x1_out[1 - u % 2], 16 * (TILES // 2))
                    sp.wait_ge(row_out[1 - u % 2], 16 * (TILES // 2))
                if u >= 0:
                    sp.wait_ge(S["x1_done"], u + 1)
                    sp.dma_start(acc[bass.ds(tile_start(u), P), :], x1[:, u % 2, :]).then_inc(x1_out[u % 2], 16)
                if t + 3 < TILES:
                    load_x(t + 3)
                if u >= 0:
                    sp.wait_ge(S["lo2_done"], u + 1)
                    sp.dma_start(rows[bass.ds(tile_start(u), P), :], row2[:, u % 2, :].bitcast(I32)
                                 ).then_inc(row_out[u % 2], 16)
            sp.wait_ge(S["brow_zero"], 1)
            sp.wait_ge(S["b12_lo"], 1)
            for j in range(2):
                sp.dma_start(brow[32 * j:32 * j + 1, :].rearrange("o (r n) -> o r n", n=D), b12[:, j, :]
                             ).then_inc(S["brow_in"], 16)
            def load_unit(e, u):
                w = w1u if u < 4 else w2u
                sp.dma_start(staging[:, u, :], w[bass.ds(4 * e + u % 4, 1), :, :].rearrange("a p n -> (a p) n")
                             ).then_inc(unit_in[u], 16)

            for u in range(RING):
                sp.wait_ge(S["lo_done"], RING + u + 1)
                load_unit(1, u)
            sp.wait_ge(S["t2_done"], TILES)
            for h in range(2):
                sp.wait_ge(row_out[h], 16 * (TILES // 2))
            for u in range(RING, UNITS):
                load_unit(1, u)
            with sp.Fori(2, E) as e:
                for u in range(UNITS):
                    sp.wait_ge(S["lo_done"], UNITS * (e - 1) + u + 1)
                    load_unit(e, u)
            tiles_used = sp.value_load(fmisc[0:1, 1, E - 1:E], min_val=E, max_val=TILES_MAX)
            sp.wait_ge(S["y_added"], 16 * tiles_used)
            sp.dma_start(out, acc[0:N, :]).then_inc(S["out_done"], 16)
            sp.wait_ge(S["out_done"], 16)

        @block.gpsimd
        def _(pool):
            pool.memset(edge_i[:, 1], FAR)
            pool.memset(edge_f[:, 1, :], 0.0).then_inc(S["pads_set"], 1)
            pool.memset(ent[:], 0).then_inc(S["mcum_zero"], 1)
            pool.memset(mcum[:, 0, :], 0.0).then_inc(S["mcum_zero"], 1)

            def split_block(j):
                pool.wait_ge(S["win_merged"], 2 * j + 2)
                pool.tensor_copy(wT[:, 0, bass.ds(j, 1), :].rearrange("p a n -> p (a n)"), wsum).then_inc(S["wsplit_hi"], 1)
                pool.wait_ge(S["wsplit_hi"], j + 1)
                hi = wT[:, 0, bass.ds(j, 1), :].rearrange("p a n -> p (a n)")
                lo = wT[:, 1, bass.ds(j, 1), :].rearrange("p a n -> p (a n)")
                pool.tensor_tensor(lo, wsum, hi, ALU.subtract).then_inc(S["wsplit_done"], 1)

            def low1(t, h):
                pool.wait_ge(S["hi1_done"], t + 1)
                pool.tensor_tensor(row1[:, h, D:2 * D], xln[:], row1[:, h, 0:D], ALU.subtract
                                   ).then_inc(S["lo1_done"], 1)

            def bias_sum(t, h):
                pool.wait_ge(x_in[h], 16 * (t // 2 + 1))
                if known(t, 2):
                    pool.wait_ge(S["x1_done"], t - 1)
                pool.tensor_tensor(xb[:, h, :], xin[:, h, :], biasb[:], ALU.add).then_inc(S["xb_done"], 1)

            pool.wait_ge(S["bcast_in"], 16)
            bias_sum(0, 0)
            low1(0, 0)
            low1(1, 1)
            with pool.Fori(0, WINS // 2) as j:
                split_block(j)

            def scatter(t, h):
                pool.wait_ge(S["slot_done"], t + 1)
                pool.wait_ge(S["gate_done"], t + 1)
                pool.sem_inc(S["pool_passed"], 1)
                for c in range(2):
                    pool.indirect_dma_start(
                        lists, bass.IndirectOffsetOnAxis(ap=slot_i[:, h, c:c + 1], axis=0), ent[:, h, c, :], None
                    ).then_inc(listed[h], 16)

            def gnn_tile(t, h):
                if below(t, TILES - 1):
                    bias_sum(t + 1, 1 - h)
                if isinstance(t, int) and t == 1:
                    pool.wait_ge(S["gnn_done"], 1)
                    pool.memset(brow, 0.0).then_inc(S["brow_zero"], 1)
                if known(t, 1) and below(t, TILES + 1):
                    low2(t - 1, 1 - h)
                if below(t, TILES - 2):
                    low1(t + 2, h)
                if known(t, 2):
                    scatter(t - 2, h)

            def low2(t, h):
                pool.wait_ge(S["hi2_done"], t + 1)
                pool.tensor_tensor(row2[:, h, D:2 * D], xln2[:], row2[:, h, 0:D], ALU.subtract
                                   ).then_inc(S["lo2_done"], 1)

            pool.wait_ge(S["lists_set"], 16)
            tiles(gnn_tile, pool)

            def gather(i):
                pool.wait_ge(S["ents_in"], 16 * (i + 1))
                if not (isinstance(i, int) and i == 0):
                    pool.wait_ge(S["xs_done"], i)
                    pool.wait_ge(S["xs_in"], 16 * i)
                pool.tensor_copy(gidx[:], ents[:, bass.ds(i & 7, 1), 0:1].rearrange("p a n -> p (a n)")
                                 ).then_inc(S["gidx_done"], 1)
                pool.wait_ge(S["gidx_done"], i + 1)
                pool.sem_inc(S["pool_passed"], 1)
                pool.indirect_dma_start(xs.bitcast(I32), None, rows, bass.IndirectOffsetOnAxis(ap=gidx[:, 0:1], axis=0)
                                        ).then_inc(S["xs_in"], 16)

            for h in range(2):
                pool.wait_ge(row_out[h], 16 * (TILES // 2))
            gather(0)
            gather(1)
            pool.wait_ge(S["table_done"], 1)
            last = pool.value_load(fmisc[0:1, 2, E - 1:E], min_val=E - 1, max_val=TILES_MAX - 1)
            for h in range(2):
                pool.wait_ge(x1_out[h], 16 * (TILES // 2))

            def add_rows(i):
                pool.wait_ge(S["y_added"], 16 * i)
                pool.tensor_copy(dest_i[:], ents[:, bass.ds(i & 7, 1), 1:2].rearrange("p a n -> p (a n)")
                                 ).then_inc(S["dest_done"], 1)
                pool.wait_ge(S["dest_done"], i + 1)
                pool.wait_ge(S["y_done"], i + 1)
                pool.sem_inc(S["pool_passed"], 1)
                pool.indirect_dma_start(acc, bass.IndirectOffsetOnAxis(ap=dest_i[:, 0:1], axis=0), yout, None,
                                        compute_op=ALU.add).then_inc(S["y_added"], 16)

            with pool.Fori(0, last) as i:
                gather(i + 2)
                add_rows(i)
            add_rows(last)

        @block.scalar
        def _(act):
            def norm1(t, h, scales):
                if known(t, 1):
                    act.wait_ge(S["lo1_done"], t)
                act.activation(xln[:], xin[:, h, :], ACT.Identity, bias=scales[:, 1:2], scale=scales[:, 0:1]
                               ).then_inc(S["xln_done"], 1)
                act.wait_ge(S["xln_done"], t + 1)
                if known(t, 2):
                    act.wait_ge(S["t1_done"], t - 1)
                act.copy(row1[:, h, 0:D], xln[:]).then_inc(S["hi1_done"], 1)

            act.wait_ge(S["stats_done"], 1)
            norm1(0, 0, ab0[:, 0])
            norm1(1, 1, ab0[:, 1])
            act.wait_ge(S["parts_done"], 1)
            act.wait_ge(S["dst1h_done"], 1)
            act.wait_ge(S["wtab_done"], 1)

            def stat_group(g):
                for k in range(GRP):
                    c = g * GRP + k
                    one = dst1h[:, bass.ds(c, 1), :].rearrange("p a n -> p (a n)")
                    to = stat[:, bass.ds(c, 1), :].rearrange("p a n -> p (a n)")
                    act.activation(to[:, 0:WIN], one, ACT.Copy, scale=whl[:, 0, bass.ds(c, 1)])
                    ins = act.activation(to[:, WIN:2 * WIN], one, ACT.Copy, scale=whl[:, 1, bass.ds(c, 1)])
                    ins.then_inc(S["stat_done"], 1)

            def stats_for(w):
                begin = act.value_load(wtab[0:1, 3, bass.ds(w, 1)], min_val=0, max_val=NCH // GRP)
                end = act.value_load(wtab[0:1, 4, bass.ds(w, 1)], min_val=0, max_val=NCH // GRP)
                with act.If(end > begin):
                    with act.Fori(begin, end) as g:
                        stat_group(within(g, 0, NCH // GRP - 1))

            def bring_low(w, h):
                groups = act.value_load(wtab[0:1, 1, bass.ds(w, 1)], min_val=2, max_val=NCH // GRP)
                before = act.value_load(wtab[0:1, 2, bass.ds(w, 1)], min_val=0, max_val=WINS * NCH // GRP)
                act.wait_ge(src1h_used[GRP - 1], before + groups + 1)
                if not (isinstance(w, int) and w == 0):
                    act.wait_ge(S["win_merged"], w)
                act.copy(wlow, psW[WIN:2 * WIN, 2 * h:2 * h + 2, :].rearrange("p a n -> p (a n)")
                         ).then_inc(S["low_brought"], 1)

            stats_for(0)
            stats_for(1)
            stats_for(2)
            bring_low(0, 0)
            with act.Fori(1, WINS // 2 - 1) as i:
                stats_for(2 * i + 1)
                bring_low(2 * i - 1, 1)
                stats_for(2 * i + 2)
                bring_low(2 * i, 0)
            stats_for(WINS - 1)
            for w in range(WINS - 3, WINS):
                bring_low(w, w % 2)

            def norm2(t, h, scales):
                if known(t, 1):
                    act.wait_ge(S["lo2_done"], t)
                act.activation(xln2[:], x1[:, h, :], ACT.Identity, bias=scales[:, 1:2], scale=scales[:, 0:1]
                               ).then_inc(S["xln2_done"], 1)
                act.wait_ge(S["xln2_done"], t + 1)
                if known(t, 2):
                    act.wait_ge(row_out[h], 16 * (t // 2))
                act.copy(row2[:, h, 0:D], xln2[:]).then_inc(S["hi2_done"], 1)

            def copy_t2(t):
                act.wait_ge(S["t2_done"], t + 1)
                if known(t, 1):
                    act.wait_ge(S["router_done"], t)
                act.copy(x2T, psT[:]).then_inc(S["t2_copied"], 1)

            def gnn_tile(t, h):
                if known(t, 2) and below(t, TILES):
                    high_unit(t - 2)
                if known(t, 2):
                    copy_t2(t - 2)
                if below(t, TILES + 1):
                    act.wait_ge(S["stats_done"], t + 2)
                if known(t, 1) and below(t, TILES + 1):
                    norm2(t - 1, 1 - h, ab[:, h, :, 1])
                if known(t, 2):
                    act.wait_ge(S["nb_done"], t - 1)
                    if known(t, 3):
                        act.wait_ge(S["gate_done"], t - 2)
                    act.activation(ex[:], m8[:, 1:2], ACT.Exp, bias=nb[:], scale=1.0 / SCALE).then_inc(S["exp_done"], 1)
                if below(t, TILES - 2):
                    norm1(t + 2, h, ab[:, h, :, 0])

            def high_unit(u):
                r = u % RING
                act.wait_ge(unit_in[r], 16 * (u // RING + 1))
                act.activation(slots[:, 0, 0, u, :], staging[:, r, :], ACT.Copy, scale=SCALE).then_inc(S["hi_done"], 1)

            for t in range(TILES + 2):
                gnn_tile(t, t % 2)

            for h in range(2):
                act.wait_ge(listed[h], 32 * (TILES // 2))

            def load_entries(i):
                row = 0 if isinstance(i, int) and i == 0 else act.value_load(
                    ftab[0:1, 1, i:i + 1] if isinstance(i, int) else ftab[0:1, 1, bass.ds(i, 1)], min_val=0,
                    max_val=DUMP + 3 * P)
                if not (isinstance(i, int) and i == 0):
                    act.wait_ge(S["ents_in"], 16 * i)
                act.dma_start(ents[:, bass.ds(i & 7, 1), :].rearrange("p a n -> p (a n)"), lists[bass.ds(row, P), :]
                              ).then_inc(S["ents_in"], 16)

            load_entries(0)
            act.wait_ge(S["table_done"], 1)
            last = act.value_load(fmisc[0:1, 2, E - 1:E], min_val=E - 1, max_val=TILES_MAX - 1)
            for i in range(1, 3):
                load_entries(i)

            def gelu(i):
                act.wait_ge(S["l1_done"], i + 1)
                act.activation(hgelu, psH, ACT.Gelu, scale=1.0 / SCALE).then_inc(S["gelu_done"], 1)
                act.wait_ge(S["gelu_done"], i + 1)
                act.copy(hsplit[:, 0, :], hgelu).then_inc(S["hhi_done"], 1)

            def gated(i):
                act.wait_ge(S["l2_done"], i + 1)
                if not (isinstance(i, int) and i == 0):
                    act.wait_ge(S["y_added"], 16 * i)
                act.activation(yout, psA[:].rearrange("p a n -> p (a n)"), ACT.Copy,
                               scale=ents[:, bass.ds(i & 7, 1), 2:3].rearrange("p a n -> p (a n)").bitcast(F32)
                               ).then_inc(S["y_done"], 1)

            def next_weights(i, units):
                fresh = act.value_load(ftab[0:1, 2, bass.ds(i, 1)], min_val=0, max_val=1)
                e = act.value_load(ftab[0:1, 0, bass.ds(i, 1)], min_val=0, max_val=E - 1)
                with act.If(fresh * (E - 1 - e) > 0):
                    for u in units:
                        act.wait_ge(unit_in[u], 16 * e + (48 if u < RING else 16))
                        to = slots[:, bass.ds((e + 1) & 1, 1), 0, u, :].rearrange("p a n -> p (a n)")
                        act.activation(to, staging[:, u, :], ACT.Copy, scale=SCALE).then_inc(S["hi_done"], 1)

            gelu(0)
            with act.Fori(0, last) as i:
                load_entries(i + 3)
                next_weights(i, range(RING))
                gelu(i + 1)
                next_weights(i, range(RING, UNITS))
                gated(i)
            gated(last)
            act.wait_ge(S["ents_in"], 16 * (last + 3))
            act.sem_inc(S["act_passed"], 1)

        @block.vector
        def _(dve):
            c_edge = Chain(dve, S["c_edge"], 10 ** 6)
            c_rng = Chain(dve, S["c_rng"], 10 ** 6)
            c_tab = Chain(dve, S["c_tab"], 10 ** 6)
            c_ln = Chain(dve, S["c_ln"], 16)
            c_rt = Chain(dve, S["c_rt"], 11)
            c_rk = Chain(dve, S["c_rk"], 4)

            def bn(src_tile, kind):
                for b in range(2):
                    c_ln.inc(dve.bn_stats(bn6[:, kind, b, :], src_tile[:, b * HALF:(b + 1) * HALF]))

            def scales(first, kinds, scale, bias):
                k = slice(first, first + kinds)
                dve.wait_ge(S["c_ln"], c_ln.base + c_ln.n)
                dve.sem_inc(S["dve_passed"], 1)
                for kind in range(first, first + kinds):
                    c_ln.inc(dve.bn_aggr(mv[:, kind, :], bn6[:, kind]))
                dve.wait_ge(S["c_ln"], c_ln.base + c_ln.n)
                m, y, z, q = (nwt[:, j, k] for j in range(4))
                c_ln.link(dve.tensor_scalar(m, mv[:, k, 1], EPS, None, ALU.add))
                c_ln.link(dve.tensor_scalar(y.bitcast(I32), m.bitcast(I32), -0.5, float(MAGIC), ALU.mult, ALU.add))
                c_ln.link(dve.tensor_tensor(z, m, y, ALU.mult))
                for three in (3.0, 12.0, 768.0):
                    c_ln.link(dve.tensor_tensor(q, z, y, ALU.mult))
                    if three < 768.0:
                        c_ln.inc(dve.scalar_tensor_tensor(z, q, -three, z, ALU.add, ALU.mult))
                    c_ln.link(dve.scalar_tensor_tensor(y, q, -three, y, ALU.add, ALU.mult))
                dve.tensor_scalar(scale, y, -1.0 / 8192, None, ALU.mult)
                dve.scalar_tensor_tensor(bias, mv[:, k, 0], 1.0 / 8192, y, ALU.mult, ALU.mult
                                         ).then_inc(S["stats_done"], 1)
                dve.sem_inc(S["c_ln"], c_ln.per - c_ln.n)
                c_ln.n = c_ln.per

            L = c_edge.link
            dve.wait_ge(S["edges_in"], 16 * 9)
            dve.wait_ge(S["consts_in"], 16 * 3)
            c_edge.start(0)
            L(dve.tensor_scalar(tmp_i, edge_i[:, :, 1, :], 6, None, ALU.arith_shift_right))
            L(dve.tensor_copy(quant[:, :, 0, :], tmp_i))
            L(dve.tensor_scalar(tmp_i, edge_i[:, :, 1, :], WIN - 1, None, ALU.bitwise_and))
            c_edge.inc(dve.tensor_copy(quant[:, :, 1, :], tmp_i))
            c_edge.inc(dve.tensor_scalar(quant[:, :, 2, :], edge_i[:, :, 0, :], 1.0, None, ALU.add))
            L(dve.tensor_scalar(quant[:, :, 3, :], edge_f, SCALE, None, ALU.mult))
            dve.engine_nop().then_inc(S["quant_done"], 1)
            R = c_rng.link
            c_rng.start(0)
            c_rng.inc(dve.tensor_reduce(bmm[:, 0, :], quant[:, :, 0, :], AX.X, ALU.min))
            R(dve.tensor_reduce(bmm[:, 1, :], quant[:, :, 0, :], AX.X, ALU.max))
            wi = k32[:, S_I16:S_I16 + WINS]
            for h in range(2):
                R(dve.tensor_scalar(touch[:, h, 0, :], wi, bmm[:, 0, h:h + 1], None, ALU.is_ge))
                R(dve.scalar_tensor_tensor(touch[:, h, 1, :], wi, bmm[:, 1, h:h + 1], touch[:, h, 0, :], ALU.is_le, ALU.mult))
                R(dve.tensor_scalar(touch[:, h, 0, :], touch[:, h, 1, :], k32[:, S_CH + h:S_CH + h + 1], -BIG,
                                    ALU.mult, ALU.add))
                R(dve.tensor_scalar(touch[:, h, 1, :], touch[:, h, 1, :], k32[:, S_CH + 2 + h:S_CH + 3 + h], None, ALU.mult))
            R(dve.tensor_tensor(lohi[:].rearrange("p (a w) -> p a w", a=2), touch[:, 0], touch[:, 1], ALU.max))
            dve.engine_nop().then_inc(S["range_done"], 1)
            dve.wait_ge(S["edges_turned"], 1)
            L(dve.tensor_copy(eT[:], psA[:].rearrange("p a n -> p (a n)").rearrange("p (q n) -> p q n", q=4)))
            L(dve.tensor_copy(whi16[:], eT[:, 3, :]))
            L(dve.tensor_copy(whl[:, 0, :], whi16[:]))
            L(dve.tensor_tensor(whl[:, 1, :], eT[:, 3, :], whl[:, 0, :], ALU.subtract))
            dve.engine_nop().then_inc(S["parts_done"], 1)
            dve.tensor_tensor(dst1h, eT[:, 1, 0:NCH].unsqueeze(2).to_broadcast([P, NCH, WIN]),
                              k32[:, S_I64:S_I64 + WIN].unsqueeze(1).to_broadcast([P, NCH, WIN]),
                              ALU.is_equal).then_inc(S["dst1h_done"], 1)
            for w in range(WINS):
                c_edge.inc(dve.scalar_tensor_tensor(srcw[:, w, :], eT[:, 0, 0:NCH], float(w), eT[:, 2, 0:NCH],
                                                    ALU.is_equal, ALU.mult))
            dve.wait_ge(S["range_turned"], 1)
            R(dve.tensor_reduce(lohiT[:], psT[0:2 * WINS, 0].rearrange("p a n -> p (a n)").bitcast(F32)[:, 0:P], AX.X, ALU.max))
            dve.engine_nop().then_inc(S["range_row"], 1)
            dve.wait_ge(S["range_turned"], 2)
            R(dve.tensor_copy(wrow[:, 0:2, :].rearrange("p a w -> p (a w)"),
                              psT[0:1, 1].rearrange("p a n -> p (a n)").bitcast(F32)[:, 0:2 * WINS]))
            R(dve.scalar_tensor_tensor(wrow[:, 2, :], wrow[:, 0, :], -1.0, wrow[:, 1, :], ALU.mult, ALU.min))
            R(dve.tensor_scalar(wrow[:, 2, :], wrow[:, 2, :], float(NCH - 2 * GRP), None, ALU.min))
            R(dve.tensor_tensor(wrow[:, 3, :], wrow[:, 1, :], wrow[:, 2, :], ALU.subtract))
            R(dve.tensor_scalar(wrow[:, 3, :], wrow[:, 3, :], float(GRP - 1), None, ALU.add))
            R(dve.tensor_copy(wtab[:, 0:2, :], wrow[:, 2:4, :]))
            R(dve.tensor_scalar(wtab[:, 1, :], wtab[:, 1, :], 2, None, ALU.arith_shift_right))
            R(dve.tensor_scalar(wtab[:, 1, :], wtab[:, 1, :], 2.0, None, ALU.max))
            R(dve.tensor_copy(wrow[:, 3, :], wtab[:, 1, :]))
            R(dve.memset(wrow[:, 5, :], 1.0))
            R(dve.tensor_tensor_scan(wrow[:, 4, :], wrow[:, 5, :], wrow[:, 3, :], 0.0, ALU.mult, ALU.add))
            R(dve.tensor_tensor(wtab[:, 2, :], wrow[:, 4, :], wrow[:, 3, :], ALU.subtract))
            R(dve.scalar_tensor_tensor(wtab[:, 4, :], wtab[:, 1, :], float(GRP), wtab[:, 0, :], ALU.mult, ALU.add))
            R(dve.tensor_scalar(wtab[:, 4, :], wtab[:, 4, :], float(GRP - 1), None, ALU.add))
            R(dve.tensor_scalar(wtab[:, 4, :], wtab[:, 4, :], 2, None, ALU.arith_shift_right))
            R(dve.tensor_copy(wrow[:, 3, :], wtab[:, 4, :]))
            R(dve.tensor_tensor_scan(wrow[:, 4, :], wrow[:, 5, :], wrow[:, 3, :], 0.0, ALU.mult, ALU.max))
            R(dve.memset(wtab[:, 3, 0:1], 0))
            R(dve.tensor_copy(wtab[:, 4, :], wrow[:, 4, :]))
            R(dve.tensor_copy(wtab[:, 3, 1:WINS], wrow[:, 4, 0:WINS - 1]))
            dve.engine_nop().then_inc(S["wtab_done"], 1)
            c_ln.start(0)
            for h in range(2):
                dve.wait_ge(x_in[h], 16)
                bn(xin[:, h, :], h)
            scales(0, 2, ab0[:, :, 0], ab0[:, :, 1])

            def onehots(g, w, c):
                for k in range(GRP):
                    dve.wait_ge(src1h_used[k], g + 1)
                    dve.tensor_scalar(ring1h[:, k, :], iota1, srcw[:, bass.ds(w, 1), bass.ds(c + k, 1)].rearrange(
                        "p a n -> p (a n)"), None, ALU.is_equal).then_inc(src1h_ready[k], 1)

            def window(w):
                first = dve.value_load(wtab[0:1, 0, bass.ds(w, 1)], min_val=0, max_val=NCH - 2 * GRP)
                groups = dve.value_load(wtab[0:1, 1, bass.ds(w, 1)], min_val=2, max_val=NCH // GRP)
                before = dve.value_load(wtab[0:1, 2, bass.ds(w, 1)], min_val=0, max_val=WINS * NCH // GRP)
                with dve.Fori(0, groups) as j:
                    onehots(before + j, w, within(first + GRP * j, 0, NCH - GRP))

            def merge(w, h):
                dve.wait_ge(S["low_brought"], w + 1)
                if h == 0 and not (isinstance(w, int) and w == 0):
                    dve.wait_ge(S["wsplit_done"], w // 2)
                dve.tensor_tensor(wsum[WIN * h:WIN * h + WIN, :],
                                  psW[0:WIN, 2 * h:2 * h + 2, :].rearrange("p a n -> p (a n)"), wlow, ALU.add
                                  ).then_inc(S["win_merged"], 1)

            window(0)
            window(1)
            merge(0, 0)
            with dve.Fori(1, WINS // 2) as i:
                window(2 * i)
                merge(2 * i - 1, 1)
                window(2 * i + 1)
                merge(2 * i, 0)
            merge(WINS - 1, 1)
            dve.wait_ge(S["biases_in"], 48)
            c_tab.start(0)
            T_ = c_tab.link
            T_(dve.tensor_scalar(rws[:, :, 0:E], rw[:], SCALE, None, ALU.mult))
            T_(dve.scalar_tensor_tensor(rws[:, :, E:2 * E], rw[:], SCALE, rws[:, :, 0:E], ALU.mult, ALU.subtract))
            T_(dve.tensor_scalar(b12[:, 0, :], brow12[:], SCALE, None, ALU.mult))
            T_(dve.scalar_tensor_tensor(b12[:, 1, :], brow12[:], SCALE, b12[:, 0, :], ALU.mult, ALU.subtract))
            dve.engine_nop().then_inc(S["rws_done"], 1)
            dve.engine_nop().then_inc(S["b12_lo"], 1)

            def copy_t1(t, h):
                dve.wait_ge(S["t1_done"], t + 1)
                if known(t, 2):
                    dve.wait_ge(S["gnn_done"], t - 1)
                dve.tensor_copy(xT[:, h], psT[:]).then_inc(S["t1_copied"], 1)

            def rank_slots(t, h):
                dve.wait_ge(S["rank_done"], t + 1)
                if known(t, 2):
                    dve.wait_ge(listed[h], 32 * (t // 2))
                c_rk.start(t)
                c_rk.link(dve.tensor_tensor(pos[:, 0, :], psK[:, 0:E], k32[:, S_EB:S_EB + E], ALU.add))
                c_rk.inc(dve.tensor_tensor(pos[:, 1, :], pos[:, 0, :], pick[:, 0, :], ALU.mult))
                c_rk.link(dve.tensor_tensor(pos[:, 2, :], pos[:, 0, :], pick[:, 1, :], ALU.mult))
                c_rk.link(dve.tensor_reduce(slotf[:], pos[:, 1:3, :], AX.X, ALU.add))
                dve.tensor_tensor(slot_i[:, h, :], slotf[:], dump_cols(t), ALU.add).then_inc(S["slot_done"], 1)

            def dump_cols(t):
                return k32[:, bass.ds(2 * t + S_DUMP, 2)]

            def mask_col(t):
                return k32[:, bass.ds(t + S_MASK, 1)]

            def entry_cols(t):
                return kdest[:, bass.ds(4 * t, 4)].rearrange("p (c a) -> p c a", a=2)

            def route(t, h):
                dve.wait_ge(S["router_done"], t + 1)
                c_rt.start(t)
                K = c_rt.link
                K(dve.tensor_copy(logit[:, 0, :], psR[:, 0:E]))
                c_rt.link_apart(dve.tensor_tensor(logit[:, 1, :], logit[:, 0, :], psR[:, E:2 * E], ALU.add), S["dve_passed"])
                c_rt.link_apart(dve.max(m8[:], logit[:, 1, :]), S["dve_passed"])
                K(dve.max_index(i8[:], m8[:], logit[:, 1, :]))
                dve.tensor_scalar(nb[:], m8[:, 0:1], -1.0 / SCALE, None, ALU.mult).then_inc(S["nb_done"], 1)
                K(dve.tensor_copy(idf[:], i8[:, 0:2]))
                c_rt.inc(dve.tensor_scalar(pick[:, 0, :], k32[:, S_I8:S_I8 + E], idf[:, 0:1], mask_col(t), ALU.is_equal, ALU.mult))
                K(dve.tensor_scalar(pick[:, 1, :], k32[:, S_I8:S_I8 + E], idf[:, 1:2], mask_col(t), ALU.is_equal, ALU.mult))
                if known(t, 1):
                    dve.wait_ge(S["rank_done"], t)
                    dve.wait_ge(S["mask_done"], t)
                K(dve.tensor_tensor(mk[:, 0, :], pick[:, 0, :], pick[:, 1, :], ALU.add))
                dve.tensor_tensor(mcum[:, 1 - h, :], mcum[:, h, :], mk[:, 0, :], ALU.add).then_inc(S["mask_done"], 1)
                dve.wait_ge(S["exp_done"], t + 1)
                if known(t, 2):
                    dve.wait_ge(listed[h], 32 * (t // 2))
                c_rt.inc(dve.tensor_copy(ent[:, h, :, 0:2], entry_cols(t)))
                K(dve.tensor_scalar(gs[:], ex[:], 1.0, SCALE, ALU.add, ALU.mult))
                K(dve.reciprocal(ent[:, h, 0, 2:3].bitcast(F32), gs[:]))
                dve.tensor_tensor(ent[:, h, 1, 2:3].bitcast(F32), ex[:], ent[:, h, 0, 2:3].bitcast(F32), ALU.mult
                                  ).then_inc(S["gate_done"], 1)

            def low_unit(t):
                dve.wait_ge(S["hi_done"], t - 1)
                u = t - 2
                hi = slots[:, 0, 0, bass.ds(u, 1), :].rearrange("p a n -> p (a n)")
                lo = slots[:, 0, 1, bass.ds(u, 1), :].rearrange("p a n -> p (a n)")
                st = staging[:, bass.ds(u % RING, 1), :].rearrange("p a n -> p (a n)")
                dve.scalar_tensor_tensor(lo, st, SCALE, hi, ALU.mult, ALU.subtract).then_inc(S["lo_done"], 1)

            def residual(t, h):
                dve.wait_ge(S["gnn_done"], t + 1)
                dve.wait_ge(S["xb_done"], t + 1)
                if known(t, 2):
                    dve.wait_ge(x1_out[h], 16 * (t // 2))
                    dve.wait_ge(S["xln2_done"], t - 1)
                dve.scalar_tensor_tensor(x1[:, h, :], psG[h], 1.0 / SCALE, xb[:, h, :],
                                         ALU.mult, ALU.add).then_inc(S["x1_done"], 1)

            def gnn_tile(t, h):
                one, two = below(t, TILES - 2), known(t, 1) and below(t, TILES + 1)
                if two:
                    residual(t - 1, 1 - h)
                if one or two:
                    c_ln.start(t + 1)
                if one:
                    dve.wait_ge(x_in[h], 16 * (t // 2 + 2))
                    bn(xin[:, h, :], 0)
                if two:
                    dve.wait_ge(S["x1_done"], t)
                    bn(x1[:, 1 - h, :], 1)
                if known(t, 2):
                    dve.wait_ge(S["xln_done"], t if below(t, TILES) and not isinstance(t, int) else min(t, TILES))
                    dve.wait_ge(S["xln2_done"], t - 2 if below(t, TILES + 2) and not isinstance(t, int) else t - 2)
                if one or two:
                    first = 0 if one else 1
                    kinds = 2 if one and two else 1
                    scales(first, kinds, ab[:, h, 0, first:first + kinds], ab[:, h, 1, first:first + kinds])
                if known(t, 2) and below(t, TILES):
                    low_unit(t)
                if known(t, 2):
                    route(t - 2, h)
                if below(t, TILES - 1):
                    copy_t1(t + 1, 1 - h)
                if known(t, 2):
                    rank_slots(t - 2, h)

            dve.wait_ge(S["mcum_zero"], 2)
            copy_t1(0, 0)
            tiles(gnn_tile, dve)
            dve.wait_ge(S["count_done"], 1)
            T_(dve.tensor_copy(cnts[:, 0, :], psR[0:1, 0:E]))
            T_(dve.tensor_scalar(cnts[:, 1, :], cnts[:, 0, :], float(P - 1), None, ALU.add))
            T_(dve.tensor_copy(cnti[:, 0, :], cnts[:, 1, :]))
            T_(dve.tensor_scalar(cnti[:, 0, :], cnti[:, 0, :], 7, None, ALU.arith_shift_right))
            T_(dve.tensor_scalar(cnts[:, 2, :], cnti[:, 0, :], 1.0, None, ALU.max))
            T_(dve.memset(cnts[:, 3, :], 1.0))
            T_(dve.tensor_tensor_scan(cnts[:, 4, :], cnts[:, 3, :], cnts[:, 2, :], 0.0, ALU.mult, ALU.add))
            T_(dve.tensor_copy(fmisc[:, 1, :], cnts[:, 4, :]))
            T_(dve.tensor_scalar(fmisc[:, 2, :], cnts[:, 4, :], -1.0, None, ALU.add))
            T_(dve.tensor_tensor(fmisc[:, 0, :], cnts[:, 0, :], k32[0:1, S_EB:S_EB + E], ALU.add))
            ti = k32[0:1, S_IT:S_IT + TMAX]
            T_(dve.tensor_tensor(tt[:, 0], ti.unsqueeze(2).to_broadcast([1, TMAX, E]),
                                 cnts[:, 4, :].unsqueeze(1).to_broadcast([1, TMAX, E]), ALU.is_ge))
            T_(dve.tensor_tensor(tt[:, 1], tt[:, 0], cnts[:, 2, :].unsqueeze(1).to_broadcast([1, TMAX, E]), ALU.mult))
            T_(dve.tensor_reduce(tf[:, 0, :], tt[:, 0], AX.X, ALU.add))
            T_(dve.tensor_reduce(tf[:, 1, :], tt[:, 1], AX.X, ALU.add))
            T_(dve.tensor_scalar(tf[:, 2, :], tf[:, 0, :], float(E - 1), None, ALU.min))
            T_(dve.tensor_copy(ftab[:, 0, :], tf[:, 2, :]))
            T_(dve.tensor_tensor(tf[:, 3, :], ti, tf[:, 1, :], ALU.subtract))
            T_(dve.tensor_scalar(ftab[:, 2, :], tf[:, 3, :], 0.0, None, ALU.is_equal))
            T_(dve.tensor_scalar(tf[:, 4, :], tf[:, 3, :], float(P), None, ALU.mult))
            T_(dve.scalar_tensor_tensor(ftab[:, 1, :], tf[:, 2, :], float(CAP), tf[:, 4, :], ALU.mult, ALU.add))
            dve.engine_nop().then_inc(S["table_done"], 1)

            last = dve.value_load(fmisc[0:1, 2, E - 1:E], min_val=E - 1, max_val=TILES_MAX - 1)

            def copy_rows(i):
                dve.wait_ge(S["xs_done"], i + 1)
                dve.tensor_copy(xsT, psT[:]).then_inc(S["xsT_copied"], 1)

            def split_h(i):
                dve.wait_ge(S["hhi_done"], i + 1)
                dve.tensor_tensor(hsplit[:, 1, :], hgelu, hsplit[:, 0, :], ALU.subtract).then_inc(S["hlo_done"], 1)

            def copy_h(i):
                dve.wait_ge(S["ht_done"], i + 1)
                dve.tensor_copy(hT[:, :, 0:FB, :], psHT).then_inc(S["ht_copied"], 1)

            copy_rows(0)
            split_h(0)
            copy_rows(1)
            copy_h(0)
            def next_weights(i, units):
                fresh = dve.value_load(ftab[0:1, 2, bass.ds(i, 1)], min_val=0, max_val=1)
                e = dve.value_load(ftab[0:1, 0, bass.ds(i, 1)], min_val=0, max_val=E - 1)
                with dve.If(fresh * (E - 1 - e) > 0):
                    for u in units:
                        dve.wait_ge(S["hi_done"], UNITS * (e + 1) + u + 1)
                        base = slots[:, bass.ds((e + 1) & 1, 1), :, u, :].rearrange("p a s n -> p (a s) n")
                        dve.scalar_tensor_tensor(base[:, 1, :], staging[:, u, :], SCALE, base[:, 0, :],
                                                 ALU.mult, ALU.subtract).then_inc(S["lo_done"], 1)

            with dve.Fori(0, last) as i:
                next_weights(i, range(RING))
                split_h(i + 1)
                copy_rows(i + 2)
                next_weights(i, range(RING, UNITS))
                copy_h(i + 1)

        @block.tensor
        def _(pe):
            pe.wait_ge(S["quant_done"], 1)
            turned = psA[:].rearrange("p a n -> p (a n)").rearrange("p (q h n) -> p q h n", q=4, h=2)
            for q in range(4):
                for h in range(2):
                    ins = pe.transpose(turned[:, q, h, :], quant[:, h, q, :], ident32)
            ins.then_inc(S["edges_turned"], 1)
            pe.wait_ge(S["range_done"], 1)
            pe.transpose(psT[0:2 * WINS, 0].rearrange("p a n -> p (a n)").bitcast(F32)[:, 0:P], lohi[:], ident32
                         ).then_inc(S["range_turned"], 1)
            pe.wait_ge(S["range_row"], 1)
            pe.transpose(psT[0:1, 1].rearrange("p a n -> p (a n)").bitcast(F32)[:, 0:2 * WINS], lohiT[:],
                         ident32[0:2 * WINS, 0:2 * WINS]).then_inc(S["range_turned"], 1)
            for k in range(GRP):
                pe.sem_inc(src1h_used[k], 1)
            pe.wait_ge(S["wtab_done"], 1)

            def group(g, c, h, start):
                for k in range(GRP):
                    pe.wait_ge(S["stat_done"], c + k + 1)
                    pe.wait_ge(src1h_ready[k], g + 1)
                    st = stat[:, bass.ds(c + k, 1), :].rearrange("p a n -> p (a n)")
                    for b in range(2):
                        ins = pe.matmul(psW[:, 2 * h + b, :], st, ring1h[:, k, b * HALF:(b + 1) * HALF],
                                        start=(start and k == 0), stop=False, skip_group_check=True)
                    ins.then_inc(src1h_used[k], 1)

            def window(w, h):
                first = pe.value_load(wtab[0:1, 0, bass.ds(w, 1)], min_val=0, max_val=NCH - 2 * GRP)
                groups = pe.value_load(wtab[0:1, 1, bass.ds(w, 1)], min_val=2, max_val=NCH // GRP)
                before = pe.value_load(wtab[0:1, 2, bass.ds(w, 1)], min_val=0, max_val=WINS * NCH // GRP)
                if not isinstance(w, int):
                    pe.wait_ge(S["win_merged"], w - 1)
                group(before, first, h, True)
                with pe.Fori(1, groups) as j:
                    group(before + j, within(first + GRP * j, 0, NCH - GRP), h, False)

            window(0, 0)
            window(1, 1)
            with pe.Fori(1, WINS // 2) as i:
                window(2 * i, 0)
                window(2 * i + 1, 1)

            def turn(rows, out_t, done):
                for part in range(2):
                    for k in range(KB):
                        ins = pe.transpose(out_t[:, part, k, :], rows[:, part * D + k * P:part * D + (k + 1) * P], ident)
                ins.then_inc(done, 1)

            def turn1(t, h):
                pe.wait_ge(S["lo1_done"], t + 1)
                if known(t, 1):
                    pe.wait_ge(S["t1_copied"], t)
                if known(t, 3):
                    pe.wait_ge(S["t2_copied"], t - 2)
                turn(row1[:, h, :], psT, S["t1_done"])

            def rank(t, h):
                pe.wait_ge(S["mask_done"], t + 1)
                if known(t, 1):
                    pe.wait_ge(S["slot_done"], t)
                pe.matmul(psK[:, 0:E], tri, mk[:, 0, :], start=True, stop=False)
                pe.matmul(psK[:, 0:E], ones, mcum[:, h, :], start=False, stop=True).then_inc(S["rank_done"], 1)

            def turn2(t, h):
                pe.wait_ge(S["lo2_done"], t + 1)
                pe.wait_ge(S["t1_copied"], t + 3 if below(t, TILES - 2) and not isinstance(t, int) else min(t + 3, TILES))
                if known(t, 1):
                    pe.wait_ge(S["t2_copied"], t)
                turn(row2[:, h, :], psT, S["t2_done"])

            def router_mm(t):
                pe.wait_ge(S["t2_copied"], t + 1)
                if known(t, 1):
                    pe.wait_ge(S["mask_done"], t)
                for part in range(2):
                    for k in range(KB):
                        ins = pe.matmul(psR[:, 0:2 * E], x2T[:, part, k, :], rws[:, k, :],
                                        start=(part == 0 and k == 0), stop=(part == 1 and k == KB - 1))
                ins.then_inc(S["router_done"], 1)

            def products(t, h, blocks):
                for k in blocks:
                    for part, wpart in ((0, 0), (0, 1), (1, 0)):
                        for b in range(2):
                            ins = pe.matmul(psG[h][:, b * HALF:(b + 1) * HALF], xT[:, h, part, k, :],
                                            wT[:, wpart, k, b * HALF:(b + 1) * HALF],
                                            start=(k == 0 and part == 0 and wpart == 0), stop=(k == KB - 1 and part == 1))
                if blocks[-1] == KB - 1:
                    ins.then_inc(S["gnn_done"], 1)

            def gnn_tile(t, h):
                now = below(t, TILES)
                if now:
                    pe.wait_ge(S["t1_copied"], t + 1)
                    if known(t, 2):
                        pe.wait_ge(S["x1_done"], t - 1)
                    products(t, h, (0, 1))
                if known(t, 2):
                    turn2(t - 2, h)
                if now:
                    products(t, h, (2, 3))
                if known(t, 2):
                    router_mm(t - 2)
                if below(t, TILES - 1):
                    turn1(t + 1, 1 - h)
                if now:
                    products(t, h, (4, 5))
                if known(t, 2):
                    rank(t - 2, h)
                if now:
                    products(t, h, (6, 7))

            pe.wait_ge(S["wsplit_done"], WINS // 2)
            pe.wait_ge(S["rws_done"], 1)
            turn1(0, 0)
            tiles(gnn_tile, pe)
            pe.wait_ge(S["mask_done"], TILES)
            pe.matmul(psR[:, 0:E], ones, mcum[:, 0, :], start=True, stop=True).then_inc(S["count_done"], 1)

            pe.wait_ge(S["table_done"], 1)
            pe.wait_ge(S["brow_in"], 32)
            last = pe.value_load(fmisc[0:1, 2, E - 1:E], min_val=E - 1, max_val=TILES_MAX - 1)

            def turn_rows(i):
                pe.wait_ge(S["xs_in"], 16 * (i + 1))
                if not (isinstance(i, int) and i == 0):
                    pe.wait_ge(S["xsT_copied"], i)
                turn(xs, psT, S["xs_done"])

            def layer1(i, e):
                pe.wait_ge(S["xsT_copied"], i + 1)
                if not (isinstance(i, int) and i == 0):
                    pe.wait_ge(S["gelu_done"], i)
                pe.wait_ge(S["lo_done"], UNITS * e + RING)
                slot = slots[:, bass.ds(e & 1, 1)].rearrange("p o a b n -> p (o a) b n")
                pe.matmul(psH, ones2, brow[:, bass.ds(e * F, F)], start=True, stop=False)
                for k in range(KB):
                    cols = slice((k % 2) * F, (k % 2) * F + F)
                    for part, wpart in ((0, 0), (0, 1), (1, 0)):
                        ins = pe.matmul(psH, xsT[:, part, k, :], slot[:, wpart, k // 2, cols],
                                        start=False, stop=(k == KB - 1 and part == 1))
                ins.then_inc(S["l1_done"], 1)

            def turn_h(i):
                pe.wait_ge(S["hlo_done"], i + 1)
                if not (isinstance(i, int) and i == 0):
                    pe.wait_ge(S["ht_copied"], i)
                for part in range(2):
                    for f in range(FB):
                        ins = pe.transpose(psHT[:, part, f, :], hsplit[:, part, f * P:(f + 1) * P], ident)
                ins.then_inc(S["ht_done"], 1)

            def layer2(i, e):
                pe.wait_ge(S["ht_copied"], i + 1)
                if not (isinstance(i, int) and i == 0):
                    pe.wait_ge(S["y_done"], i)
                pe.wait_ge(S["lo_done"], UNITS * e + UNITS)
                slot = slots[:, bass.ds(e & 1, 1)].rearrange("p o a b n -> p (o a) b n")
                for b in range(2):
                    pe.matmul(psA[:, b, :], ones2, brow[:, bass.ds(E * F + e * D + b * HALF, HALF)], start=True, stop=False)
                for f in range(FB):
                    for part, wpart in ((0, 0), (0, 1), (1, 0)):
                        for b in range(2):
                            ins = pe.matmul(psA[:, b, :], hT[:, part, f, :], slot[:, wpart, 4 + f, b * HALF:(b + 1) * HALF],
                                            start=False, stop=(f == FB - 1 and part == 1))
                ins.then_inc(S["l2_done"], 1)

            turn_rows(0)
            layer1(0, 0)
            turn_rows(1)
            turn_h(0)
            with pe.Fori(0, last) as i:
                e0 = pe.value_load(ftab[0:1, 0, bass.ds(i, 1)], min_val=0, max_val=E - 1)
                e1 = pe.value_load(ftab[0:1, 0, bass.ds(i + 1, 1)], min_val=0, max_val=E - 1)
                layer1(i + 1, e1)
                turn_rows(i + 2)
                layer2(i, e0)
                turn_h(i + 1)
            layer2(last, E - 1)


def constants(np):
    p = np.arange(P)
    k16 = np.zeros((P, H_END), np.float16)
    k16[:, H_ID:H_ID + P] = np.eye(P)
    k16[:, H_TRI:H_TRI + P] = p[:, None] < p[None, :]
    k16[:, H_ONE:H_ONE + P] = 1
    k16[0, H_ONE2:H_ONE2 + P] = 1
    k16[32, H_ONE2:H_ONE2 + P] = 1
    k16[:, H_IOTA:H_IOTA + D] = np.arange(1, D + 1)
    k32 = np.zeros((P, S_END), np.float32)
    k32[:, S_ID:S_ID + P] = np.eye(P)
    k32[:, S_I64:S_I64 + WIN] = np.arange(WIN)
    k32[:, S_I16:S_I16 + WINS] = np.arange(WINS)
    k32[:, S_I8:S_I8 + E] = np.arange(E)
    for h in range(2):
        k32[:, S_CH + h] = BIG - (p + P * h)
        k32[:, S_CH + 2 + h] = p + P * h + 1
    k32[:, S_EB:S_EB + E] = np.arange(E) * CAP
    k32[:, S_MASK:S_MASK + TILES] = 1
    k32[:REPEAT, S_MASK + TILES - 1] = 0
    for c in range(2):
        k32[:REPEAT, S_DUMP + 2 * (TILES - 1) + c] = DUMP + P * c + p[:REPEAT]
    k32[:, S_IT:S_IT + TMAX] = np.arange(TMAX)
    k32[:, S_SC] = SCALE
    kd = np.zeros((P, TILES, 2, 2), np.int32)
    for t in range(TILES):
        kd[:, t] = (min(P * t, LAST) + p)[:, None, None]
    kd = kd.reshape(P, 4 * TILES)
    pads = np.zeros((DUMP + 4 * P, 4), np.int32)
    pads[:, 1] = N + np.arange(DUMP + 4 * P) % P
    return k16, k32, kd, pads


def kernel(x, src, dst, edge_weight, L0_gnn_bias, L0_ffn_router_w, L0_ffn_w1, L0_ffn_b1, L0_ffn_w2, L0_ffn_b2):
    import numpy as np
    import concourse.bacc as bacc
    from concourse.bass_utils import run_bass_kernel_spmd

    def lay(a):
        return np.ascontiguousarray(a)

    k16, k32, kd, pads = constants(np)
    w1 = np.asarray(L0_ffn_w1).transpose(0, 2, 1).reshape(E, UNITS // 2, 2, P, F).transpose(0, 1, 3, 2, 4)
    w2 = np.asarray(L0_ffn_w2).transpose(0, 2, 1)
    arrays = {
        "x": lay(x), "src": lay(src), "dst": lay(dst), "edge_w": lay(edge_weight),
        "bias": lay(np.asarray(L0_gnn_bias).reshape(1, D)),
        "router": lay(np.asarray(L0_ffn_router_w).reshape(E, KB, P).transpose(2, 1, 0)),
        "w1u": lay(w1.reshape(E * UNITS // 2, P, 2 * F)), "w2u": lay(w2.reshape(E * FB, P, D)),
        "b1": lay(np.asarray(L0_ffn_b1).reshape(E * F // D, D)), "b2": lay(L0_ffn_b2),
        "c16": k16, "c32": k32, "ci": kd, "cl": pads,
    }
    nc = bacc.Bacc("TRN2", target_bir_lowering=False, num_devices=1)
    args = {name: nc.dram_tensor(name, a.shape, mybir.dt.from_np(a.dtype), kind="ExternalInput").ap()
            for name, a in arrays.items()}
    out = nc.dram_tensor("out", (N, D), F32, kind="ExternalOutput").ap()
    build_program(nc, out=out, **args)
    r = run_bass_kernel_spmd(nc, [arrays], core_ids=[0])
    return r.results[0]["out"]
```

```python
from contextlib import ExitStack

import concourse.bass as bass
from concourse import mybir

ALU = mybir.AluOpType
ACT = mybir.ActivationFunctionType
AX = mybir.AxisListType
F32 = mybir.dt.float32
F16 = mybir.dt.float16
I32 = mybir.dt.int32
U32 = mybir.dt.uint32

P = 128
N = 1250
D = 1024
KB = D // P
NE = 21250
E = 8
F = 512
FB = F // P
HALF = 512
EPS = 1e-5
SCALE = 64.0
TILES = (N + P - 1) // P
LAST = N - P
REPEAT = P * TILES - N

WIN = 64
WINS = D // WIN
GRP = 4
LEAST = 3
NCH = ((NE + P - 1) // P + 2 * GRP - 1) // GRP * GRP
FAR = 2 ** 20
BIG = 512.0

CAP = N // P * P + 2 * P
DUMP = E * CAP
TILES_MAX = (2 * N + E * (P - 1)) // P
TMAX = 32
UNITS = 8
RING = UNITS // 2
MAGIC = 0x5F3759DF

H_ID, H_TRI, H_ONE, H_IOTA, H_END = 0, 128, 256, 384, 384 + D
S_ID, S_I64, S_I16, S_I8, S_CH, S_EB, S_MASK, S_DUMP, S_IT, S_END = (
    0, 128, 192, 208, 216, 220, 228, 238, 258, 290)


class Chain:

    def __init__(self, eng, sem, per):
        self.eng, self.sem, self.per, self.base, self.n = eng, sem, per, 0, 0

    def start(self, index):
        assert self.n in (0, self.per), (self.n, self.per)
        self.base, self.n = index * self.per, 0

    def inc(self, ins):
        self.n += 1
        ins.then_inc(self.sem, 1)

    def link(self, ins):
        self.inc(ins)
        self.eng.wait_ge(self.sem, self.base + self.n)

    def link_apart(self, ins, passed):
        self.link(ins)
        self.eng.sem_inc(passed, 1)


def build_program(nc, x, src, dst, edge_w, bias, router, w1u, w2u, b1, b2, c16, c32, ci, cl, out):
    ctx = ExitStack()
    with ctx:
        def sb(name, shape, dt):
            return ctx.enter_context(nc.sbuf_tensor(name, shape, dt))

        def sem(name):
            return ctx.enter_context(nc.semaphore(name))

        lists = nc.dram_tensor("lists", [DUMP + 4 * P, 4], I32).ap()
        rows = nc.dram_tensor("rows", [N, D], I32).ap()
        acc = nc.dram_tensor("acc", [N + P, D], F32).ap()

        k16 = sb("k16", [P, H_END], F16)
        k32 = sb("k32", [P, S_END], F32)
        kdest = sb("kdest", [P, 4 * TILES], I32)
        slots = sb("slots", [P, 2, 2, UNITS, D], F16)
        wT = slots[:, 1]
        dst1h = slots[:, 0].rearrange("p a b c -> p (a b c)")[:, 0:NCH * WIN].rearrange("p (c n) -> p c n", n=WIN)
        late = sb("late", [P, NCH * 2 * WIN], F16)
        stat = late[:].rearrange("p (c n) -> p c n", n=2 * WIN)
        ffn_bias = late[:, 0:8 * (F + D)].bitcast(F32).rearrange("p (e n) -> p e n", e=4)
        xs = late[:, 8 * (F + D):8 * (F + D) + 2 * D]
        staging = sb("staging", [P, UNITS, D], F32)
        rows16 = staging[:, RING:UNITS, :].rearrange("p r n -> p (r n)").bitcast(F16).rearrange(
            "p (a h n) -> p a h n", a=2, h=2)
        ring1h = sb("ring1h", [P, 2 * GRP, D], F16)
        x1 = ring1h[:].rearrange("p r n -> p (r n)").bitcast(F32)[:, 0:2 * D].rearrange("p (r n) -> p r n", n=D)
        spare = ring1h[:, GRP:2 * GRP, :].rearrange("p r n -> p (r n)").bitcast(F32)
        quant = spare[:, 0:8 * P].rearrange("p (h q n) -> p h q n", h=2, q=4)
        tt = spare[0:1, D:D + 2 * TMAX * E].rearrange("p (a i e) -> p a i e", a=2, e=E)
        xin = sb("xin", [P, 2, D], F32)
        xb = sb("xb", [P, 2, D], F32)
        yout = xb[:, 0]
        hgelu = xb[:, 1, 0:F]
        hsplit = xb[:, 1].bitcast(F16)[:, 2 * F:4 * F].rearrange("p (s n) -> p s n", s=2)
        hsum = xin[:, 1, 0:F]
        biasb = sb("biasb", [P, D], F32)
        xln = sb("xln", [P, D], F32)
        ysum = xln[:]
        xln2 = sb("xln2", [P, D], F32)
        wsum = xln2[:]
        row1 = rows16[:, 0]
        row2 = rows16[:, 1]
        xTs = sb("xTs", [P, 3, 2, KB, P], F16)
        xT = xTs[:, 0:2]
        x2T = xTs[:, 2]
        srcw_flat = xTs[:].rearrange("p a b c d -> p (a b c d)").bitcast(F32)[:, 0:WINS * NCH]
        srcw = srcw_flat.rearrange("p (w c) -> p w c", w=WINS)
        xsT = x2T
        hT = xTs[:, 0]
        edge_i = xln2[:, 0:4 * P].bitcast(I32).rearrange("p (h j e) -> p h j e", h=2, j=2)
        edge_f = xln2[:, 4 * P:6 * P].rearrange("p (h e) -> p h e", h=2)
        tmp_i = xln2[:, 6 * P:8 * P].bitcast(I32).rearrange("p (h e) -> p h e", h=2)
        behind = slots[:, 0].rearrange("p a b c -> p (a b c)")[:, NCH * WIN:].bitcast(F32)
        eT = behind[:, 0:8 * P].rearrange("p (q n) -> p q n", q=4)
        whl = behind[:, 8 * P:12 * P].rearrange("p (a n) -> p a n", a=2)
        whi16 = sb("whi16", [P, 2 * P], F16)
        bmm = sb("bmm", [P, 2, 2], F32)
        touch = sb("touch", [P, 2, 2, WINS], F32)
        lohi = sb("lohi", [P, 2 * WINS], F32)
        lohiT = sb("lohiT", [2 * WINS, 1], F32)
        wrow = sb("wrow", [1, 6, WINS], F32)
        wtab = sb("wtab", [1, 5, WINS], I32)
        wpack = sb("wpack", [1, 2, WINS], I32)
        wlow = row2[:, 1, :].bitcast(F32)
        whigh = xb[:, 1, :]
        rw = sb("rw", [P, KB, E], F32)
        rws = sb("rws", [P, KB, 2 * E], F16)
        bn6 = sb("bn6", [P, 2, 2, 6], F32)
        mv = sb("mv", [P, 2, 2], F32)
        nwt = sb("nwt", [P, 5, 2], F32)
        ab0 = sb("ab0", [P, 2, 2], F32)
        ab = sb("ab", [P, 2, 2, 2], F32)
        logit = sb("logit", [P, 2, E], F32)
        m8 = sb("m8", [P, 8], F32)
        i8 = sb("i8", [P, 8], U32)
        idf = sb("idf", [P, 2], F32)
        nb = sb("nb", [P, 1], F32)
        ex = sb("ex", [P, 1], F32)
        gs = sb("gs", [P, 1], F32)
        ent = sb("ent", [P, 2, 2, 4], I32)
        pick = sb("pick", [P, 2, E], F32)
        mk = sb("mk", [P, 2, E], F16)
        mcum = sb("mcum", [P, 2, E], F16)
        pos = sb("pos", [P, 3, E], F32)
        slotf = sb("slotf", [P, 2], F32)
        slot_i = sb("slot_i", [P, 2, 2], I32)
        cnts = sb("cnts", [1, 6, E], F32)
        cnti = sb("cnti", [1, E], I32)
        tf = sb("tf", [1, 6, TMAX], F32)
        ftab = sb("ftab", [1, 2, TMAX], I32)
        last_tile = sb("last_tile", [1, E], I32)
        before = sb("before", [1, TILES + 1], F32)
        needed = sb("needed", [1, TILES], I32)
        ents = sb("ents", [P, 8, 4], I32)
        gidx = sb("gidx", [P, 1], I32)
        dest_i = sb("dest_i", [P, 1], I32)

        psA = ctx.enter_context(nc.psum_tensor("psA", [P, 2, HALF], F32))
        psT = ctx.enter_context(nc.psum_tensor("psT", [P, 2, KB, P], F16))
        psW = ctx.enter_context(nc.psum_tensor("psW", [P, 4, HALF], F32))
        psG = (psA[:].rearrange("p a n -> p (a n)"), psW[:, 2:4, :].rearrange("p a n -> p (a n)"))
        psR = psW[:, 0]
        psK = psW[:, 1]
        psH = psW[:, 2]
        psHT = psW[:, 3].bitcast(F16).rearrange("p (s f n) -> p s f n", s=2, f=FB)

        s = {}
        for name in """k32_in consts_in edges_in biases_in ffn_bias_in bcast_in pads_set quant_done edges_turned
                       parts_done dst1h_done wtab_done range_turned range_done range_row stat_hi_done stat_lo_done
                       win_merged dve_passed pool_passed act_passed sp_passed brought wsplit_done
                       xln_done hi1_done lo1_done xb_done t1_done t1_copied
                       gnn_done x1_done stats_done xln2_done hi2_done lo2_done t2_done t2_copied low_copied
                       router_done
                       nb_done exp_done gate_done mask_done rank_done slot_done count_done table_done needed_done
                       rws_done lists_set mcum_zero wsplit_hi gidx_done
                       lo_done hi_done ents_in xs_in xs_done l1_done hsum_done gelu_done hhi_done hlo_done
                       ht_done ht_copied l2_done
                       ysum_done y_done dest_done y_added out_done
                       xsT_copied c_edge c_rng c_ln c_rt c_rk c_tab""".split():
            s[name] = sem(name)
        S = s
        src1h_ready = [sem(f"src1h_ready{g}") for g in range(GRP)]
        src1h_used = [sem(f"src1h_used{g}") for g in range(GRP)]
        x_in = [sem(f"x_in{h}") for h in range(2)]
        x1_out = [sem(f"x1_out{h}") for h in range(2)]
        row_out = [sem(f"row_out{h}") for h in range(2)]
        listed = [sem(f"listed{h}") for h in range(2)]
        unit_in = [sem(f"unit_in{r}") for r in range(UNITS)]

        ident = k16[:, H_ID:H_ID + P]
        tri = k16[:, H_TRI:H_TRI + P]
        ones = k16[:, H_ONE:H_ONE + P]
        iota1 = k16[:, H_IOTA:H_IOTA + D]
        ident32 = k32[:, S_ID:S_ID + P]

        def tile_start(t):
            return P * t - REPEAT * (t // (TILES - 1))

        def tiles(body, eng):
            body(0, 0)
            body(1, 1)
            with eng.Fori(1, TILES // 2 - 1) as i:
                body(2 * i, 0)
                body(2 * i + 1, 1)
            for t in range(TILES - 2, TILES + 2):
                body(t, t % 2)

        def within(v, low, high):
            return v if isinstance(v, int) else v.with_bounds(min_val=low, max_val=high)

        def known(t, low):
            return t >= low if isinstance(t, int) else True

        def below(t, high):
            return t < high if isinstance(t, int) else True

        def stats_for(eng, w, stat_group):
            both = eng.value_load(wpack[0:1, 1, bass.ds(w, 1)], min_val=0, max_val=2 ** 12)
            begin, end = within(both >> 6, 0, NCH // GRP), within(both & 63, 0, NCH // GRP)
            with eng.If(end > begin):
                with eng.Fori(begin, end) as g:
                    stat_group(within(g, 0, NCH // GRP - 1))

        def experts_of(eng, i):
            v = eng.value_load(ftab[0:1, 0, bass.ds(i, 1)], min_val=0, max_val=127)
            return within(v & 7, 0, E - 1), within(v >> 4, 0, E - 1), (v & 8) > 0

        def window_range(eng, w):
            v = eng.value_load(wpack[0:1, 0, bass.ds(w, 1)], min_val=2, max_val=2 ** 24)
            return (within((v >> 6) & 255, 0, NCH - LEAST * GRP), within(v & 63, LEAST, NCH // GRP),
                    within(v >> 14, 0, WINS * NCH // GRP))

        block = ctx.enter_context(nc.Block())

        @block.sync
        def _(sp):
            full = NE // P - P
            rest = NE - (P + full) * P
            sp.dma_start(k32[:], c32).then_inc(S["k32_in"], 16)
            for j, a in enumerate((src, dst)):
                sp.dma_start(edge_i[:, 0, j, :], a[0:P * P].rearrange("(c e) -> c e", e=P)).then_inc(S["edges_in"], 16)
            sp.dma_start(edge_f[:, 0, :], edge_w[0:P * P].rearrange("(c e) -> c e", e=P)).then_inc(S["edges_in"], 16)
            sp.wait_ge(S["pads_set"], 1)
            for j, a in enumerate((src, dst)):
                sp.dma_start(edge_i[0:full, 1, j, :],
                             a[P * P:(P + full) * P].rearrange("(c e) -> c e", e=P)).then_inc(S["edges_in"], 16)
                sp.dma_start(edge_i[full:full + 1, 1, j, 0:rest],
                             a[(P + full) * P:NE].rearrange("(c e) -> c e", c=1)).then_inc(S["edges_in"], 16)
            sp.dma_start(edge_f[0:full, 1, :],
                         edge_w[P * P:(P + full) * P].rearrange("(c e) -> c e", e=P)).then_inc(S["edges_in"], 16)
            sp.dma_start(edge_f[full:full + 1, 1, 0:rest],
                         edge_w[(P + full) * P:NE].rearrange("(c e) -> c e", c=1)).then_inc(S["edges_in"], 16)
            sp.dma_start(k16[:], c16).then_inc(S["consts_in"], 16)
            sp.dma_start(kdest[:], ci).then_inc(S["consts_in"], 16)
            sp.dma_start(rw[:], router).then_inc(S["biases_in"], 16)
            for r in range(RING):
                sp.dma_start(staging[:, r, :], w1u[r, :, :]).then_inc(unit_in[r], 16)
            sp.dma_start(lists, cl).then_inc(S["lists_set"], 16)

            def load_x(t):
                sp.wait_ge(S["xb_done"], t - 1)
                sp.wait_ge(S["xln_done"], t - 1)
                sp.dma_start(xin[:, t % 2, :], x[bass.ds(tile_start(t), P), :]).then_inc(x_in[t % 2], 16)

            def load_unit(e, u, place):
                w = w1u if u < 4 else w2u
                sp.dma_start(staging[:, place, :], w[bass.ds(4 * e + u % 4, 1), :, :].rearrange("a p n -> (a p) n")
                             ).then_inc(unit_in[place], 16)

            def load_bias(e):
                if not (isinstance(e, int) and e == 0):
                    sp.wait_ge(S["ffn_bias_in"], 32 * e)
                    sp.sem_inc(S["sp_passed"], 1)
                place = ffn_bias[:, bass.ds(e & 3, 1), :].rearrange("p a n -> p (a n)")
                sp.dma_start(place[:, 0:F], b1[bass.ds(e, 1), :].to_broadcast([P, F])).then_inc(S["ffn_bias_in"], 16)
                sp.dma_start(place[:, F:F + D], b2[bass.ds(e, 1), :].to_broadcast([P, D])
                             ).then_inc(S["ffn_bias_in"], 16)

            load_x(2)
            for t in range(TILES + 1):
                if 4 <= t < 4 + RING:
                    sp.wait_ge(S["lo_done"], t - 3)
                    load_unit(0, t, t - 4)
                if 7 <= t:
                    sp.wait_ge(S["lo_done"], t - 2)
                    load_unit(1, t - 7, t - 7)
                u = t - 1
                if u == TILES - 1:
                    sp.wait_ge(x1_out[1 - u % 2], 16 * (TILES // 2))
                    sp.wait_ge(row_out[1 - u % 2], 16 * (TILES // 2))
                if u >= 0:
                    sp.wait_ge(S["x1_done"], u + 1)
                    sp.dma_start(acc[bass.ds(tile_start(u), P), :], x1[:, u % 2, :]).then_inc(x1_out[u % 2], 16)
                if t + 3 < TILES:
                    load_x(t + 3)
                if t in (2, 3):
                    load_bias(t - 2)
                if u >= 0:
                    sp.wait_ge(S["lo2_done"], u + 1)
                    sp.dma_start(rows[bass.ds(tile_start(u), P), :], row2[:, u % 2, :].bitcast(I32)
                                 ).then_inc(row_out[u % 2], 16)
            sp.wait_ge(S["t2_done"], TILES)
            for h in range(2):
                sp.wait_ge(row_out[h], 16 * (TILES // 2))
            sp.wait_ge(S["xs_in"], 16)
            for u in range(RING, UNITS):
                load_unit(1, u, u)
            with sp.Fori(2, E) as e:
                for u in range(UNITS):
                    sp.wait_ge(S["lo_done"], UNITS * (e - 1) + u + 1)
                    load_unit(e, u, u)
                load_bias(e)
            sp.wait_ge(S["needed_done"], 1)
            with sp.Fori(0, TILES - 1) as t:
                tiles_needed = sp.value_load(needed[0:1, bass.ds(t, 1)], min_val=E - 1, max_val=TILES_MAX)
                sp.wait_ge(S["y_added"], 16 * tiles_needed)
                start = within(P * t, 0, N - P)
                sp.dma_start(out[bass.ds(start, P), :], acc[bass.ds(start, P), :]).then_inc(S["out_done"], 16)
            start = P * (TILES - 1)
            sp.wait_ge(S["y_added"], 16 * sp.value_load(needed[0:1, TILES - 1:TILES],
                                                        min_val=E - 1, max_val=TILES_MAX))
            sp.dma_start(out[start:N, :], acc[start:N, :]).then_inc(S["out_done"], 16)
            sp.wait_ge(S["out_done"], 16 * TILES)

        @block.gpsimd
        def _(pool):
            pool.memset(edge_i[:, 1], FAR)
            pool.memset(edge_f[:, 1, :], 0.0).then_inc(S["pads_set"], 1)
            pool.memset(ent[:], 0).then_inc(S["mcum_zero"], 1)
            pool.memset(mcum[:, 0, :], 0.0).then_inc(S["mcum_zero"], 1)

            def stat_group(g):
                shape = [P, GRP, WIN]
                pool.tensor_tensor(stat[:, bass.ds(GRP * g, GRP), WIN:2 * WIN], dst1h[:, bass.ds(GRP * g, GRP), :],
                                   whl[:, 1, bass.ds(GRP * g, GRP)].unsqueeze(2).to_broadcast(shape), ALU.mult
                                   ).then_inc(S["stat_lo_done"], GRP)

            def merge(j):
                pool.wait_ge(S["brought"], 2 * j + 2)
                if not isinstance(j, int) or j > 0:
                    pool.wait_ge(S["wsplit_done"], j)
                pool.tensor_tensor(wsum, whigh, wlow, ALU.add).then_inc(S["win_merged"], 1)

            def split_low(j):
                pool.wait_ge(S["wsplit_hi"], j + 1)
                hi = wT[:, 0, bass.ds(j, 1), :].rearrange("p a n -> p (a n)")
                lo = wT[:, 1, bass.ds(j, 1), :].rearrange("p a n -> p (a n)")
                pool.tensor_tensor(lo, wsum, hi, ALU.subtract).then_inc(S["wsplit_done"], 1)

            def low1(t, h):
                pool.wait_ge(S["hi1_done"], t + 1)
                pool.tensor_tensor(row1[:, h, D:2 * D], xln[:], row1[:, h, 0:D], ALU.subtract
                                   ).then_inc(S["lo1_done"], 1)

            def bias_sum(t, h):
                pool.wait_ge(x_in[h], 16 * (t // 2 + 1))
                if known(t, 2):
                    pool.wait_ge(S["x1_done"], t - 1)
                pool.tensor_tensor(xb[:, h, :], xin[:, h, :], biasb[:], ALU.add).then_inc(S["xb_done"], 1)

            pool.wait_ge(S["bcast_in"], 16)
            bias_sum(0, 0)
            low1(0, 0)
            low1(1, 1)
            pool.wait_ge(S["parts_done"], 1)
            pool.wait_ge(S["dst1h_done"], 1)
            pool.wait_ge(S["wtab_done"], 1)
            for w in range(3):
                stats_for(pool, w, stat_group)
            with pool.Fori(1, WINS // 2 - 1) as i:
                stats_for(pool, 2 * i + 1, stat_group)
                merge(i - 1)
                stats_for(pool, 2 * i + 2, stat_group)
                split_low(i - 1)
            stats_for(pool, WINS - 1, stat_group)
            for j in (WINS // 2 - 2, WINS // 2 - 1):
                merge(j)
                split_low(j)

            def scatter(t, h):
                pool.wait_ge(S["slot_done"], t + 1)
                pool.wait_ge(S["gate_done"], t + 1)
                pool.sem_inc(S["pool_passed"], 1)
                for c in range(2):
                    pool.indirect_dma_start(
                        lists, bass.IndirectOffsetOnAxis(ap=slot_i[:, h, c:c + 1], axis=0), ent[:, h, c, :], None
                    ).then_inc(listed[h], 16)

            def gnn_tile(t, h):
                if below(t, TILES - 1):
                    bias_sum(t + 1, 1 - h)
                if known(t, 1) and below(t, TILES + 1):
                    low2(t - 1, 1 - h)
                if below(t, TILES - 2):
                    low1(t + 2, h)
                if known(t, 2):
                    scatter(t - 2, h)

            def low2(t, h):
                pool.wait_ge(S["hi2_done"], t + 1)
                pool.tensor_tensor(row2[:, h, D:2 * D], xln2[:], row2[:, h, 0:D], ALU.subtract
                                   ).then_inc(S["lo2_done"], 1)

            pool.wait_ge(S["lists_set"], 16)
            tiles(gnn_tile, pool)

            def gather(i):
                pool.wait_ge(S["ents_in"], 16 * (i + 1))
                if not (isinstance(i, int) and i == 0):
                    pool.wait_ge(S["xs_done"], i)
                    pool.wait_ge(S["xs_in"], 16 * i)
                pool.tensor_copy(gidx[:], ents[:, bass.ds(i & 7, 1), 0:1].rearrange("p a n -> p (a n)")
                                 ).then_inc(S["gidx_done"], 1)
                pool.wait_ge(S["gidx_done"], i + 1)
                pool.sem_inc(S["pool_passed"], 1)
                pool.indirect_dma_start(xs.bitcast(I32), None, rows, bass.IndirectOffsetOnAxis(ap=gidx[:, 0:1], axis=0)
                                        ).then_inc(S["xs_in"], 16)

            for h in range(2):
                pool.wait_ge(row_out[h], 16 * (TILES // 2))
            gather(0)
            gather(1)
            gather(2)
            pool.wait_ge(S["table_done"], 1)
            last = pool.value_load(last_tile[0:1, E - 1:E], min_val=E - 1, max_val=TILES_MAX - 1)
            for h in range(2):
                pool.wait_ge(x1_out[h], 16 * (TILES // 2))

            def add_rows(i):
                pool.wait_ge(S["y_added"], 16 * i)
                pool.tensor_copy(dest_i[:], ents[:, bass.ds(i & 7, 1), 1:2].rearrange("p a n -> p (a n)")
                                 ).then_inc(S["dest_done"], 1)
                pool.wait_ge(S["dest_done"], i + 1)
                pool.wait_ge(S["y_done"], i + 1)
                pool.sem_inc(S["pool_passed"], 1)
                pool.indirect_dma_start(acc, bass.IndirectOffsetOnAxis(ap=dest_i[:, 0:1], axis=0), yout, None,
                                        compute_op=ALU.add).then_inc(S["y_added"], 16)

            with pool.Fori(0, last) as i:
                gather(i + 3)
                add_rows(i)
            add_rows(last)

        @block.scalar
        def _(act):
            def norm1(t, h, scales):
                if known(t, 1):
                    act.wait_ge(S["lo1_done"], t)
                act.activation(xln[:], xin[:, h, :], ACT.Identity, bias=scales[:, 1:2], scale=scales[:, 0:1]
                               ).then_inc(S["xln_done"], 1)
                act.wait_ge(S["xln_done"], t + 1)
                if known(t, 2):
                    act.wait_ge(S["t1_done"], t - 1)
                act.copy(row1[:, h, 0:D], xln[:]).then_inc(S["hi1_done"], 1)

            for h in range(2):
                act.dma_start(xin[:, h, :], x[h * P:(h + 1) * P, :]).then_inc(x_in[h], 16)
            act.dma_start(biasb[:], bias.to_broadcast([P, D])).then_inc(S["bcast_in"], 16)
            act.wait_ge(S["stats_done"], 1)
            norm1(0, 0, ab0[:, 0])
            norm1(1, 1, ab0[:, 1])
            act.wait_ge(S["parts_done"], 1)
            act.wait_ge(S["dst1h_done"], 1)
            act.wait_ge(S["wtab_done"], 1)

            def stat_group(g):
                one4, to4 = dst1h[:, bass.ds(GRP * g, GRP), :], stat[:, bass.ds(GRP * g, GRP), :]
                w4 = whl[:, 0, bass.ds(GRP * g, GRP)]
                for k in range(GRP):
                    ins = act.activation(to4[:, k, 0:WIN], one4[:, k, :], ACT.Copy, scale=w4[:, k:k + 1])
                ins.then_inc(S["stat_hi_done"], GRP)

            def bring(w, h):
                _, groups, before = window_range(act, w)
                act.wait_ge(src1h_used[GRP - 1], before + groups + 2)
                if h == 0 and not (isinstance(w, int) and w == 0):
                    act.wait_ge(S["win_merged"], w // 2)
                here = slice(WIN * h, WIN * h + WIN)
                act.copy(whigh[here], psW[0:WIN, 2 * h:2 * h + 2, :].rearrange("p a n -> p (a n)"))
                act.copy(wlow[here], psW[WIN:2 * WIN, 2 * h:2 * h + 2, :].rearrange("p a n -> p (a n)")
                         ).then_inc(S["brought"], 1)

            def split_high(j):
                act.wait_ge(S["win_merged"], j + 1)
                act.copy(wT[:, 0, bass.ds(j, 1), :].rearrange("p a n -> p (a n)"), wsum).then_inc(S["wsplit_hi"], 1)

            for w in range(3):
                stats_for(act, w, stat_group)
            bring(0, 0)
            with act.Fori(1, WINS // 2 - 1) as i:
                stats_for(act, 2 * i + 1, stat_group)
                bring(2 * i - 1, 1)
                stats_for(act, 2 * i + 2, stat_group)
                split_high(i - 1)
                bring(2 * i, 0)
            stats_for(act, WINS - 1, stat_group)
            bring(WINS - 3, 1)
            split_high(WINS // 2 - 2)
            bring(WINS - 2, 0)
            bring(WINS - 1, 1)
            split_high(WINS // 2 - 1)

            def norm2(t, h, scales):
                if known(t, 1):
                    act.wait_ge(S["lo2_done"], t)
                act.activation(xln2[:], x1[:, h, :], ACT.Identity, bias=scales[:, 1:2], scale=scales[:, 0:1]
                               ).then_inc(S["xln2_done"], 1)
                act.wait_ge(S["xln2_done"], t + 1)
                if known(t, 2):
                    act.wait_ge(row_out[h], 16 * (t // 2))
                act.copy(row2[:, h, 0:D], xln2[:]).then_inc(S["hi2_done"], 1)

            def copy_t2(t):
                act.wait_ge(S["t2_done"], t + 1)
                if known(t, 1):
                    act.wait_ge(S["router_done"], t)
                if isinstance(t, int) and t == TILES - 1:
                    act.copy(x2T[:, 0], psT[:, 0]).then_inc(S["t2_copied"], 1)
                else:
                    act.copy(x2T, psT[:]).then_inc(S["t2_copied"], 1)

            def gnn_tile(t, h):
                if known(t, 2) and below(t, TILES):
                    high_unit(t - 2)
                if known(t, 2):
                    copy_t2(t - 2)
                if below(t, TILES + 1):
                    act.wait_ge(S["stats_done"], t + 2)
                if known(t, 1) and below(t, TILES + 1):
                    norm2(t - 1, 1 - h, ab[:, h, :, 1])
                if known(t, 2):
                    act.wait_ge(S["nb_done"], t - 1)
                    if known(t, 3):
                        act.wait_ge(S["gate_done"], t - 2)
                    act.activation(ex[:], m8[:, 1:2], ACT.Exp, bias=nb[:], scale=1.0 / SCALE).then_inc(S["exp_done"], 1)
                if below(t, TILES - 2):
                    norm1(t + 2, h, ab[:, h, :, 0])

            def high_unit(u):
                r = u % RING
                act.wait_ge(unit_in[r], 16 * (u // RING + 1))
                act.activation(slots[:, 0, 0, u, :], staging[:, r, :], ACT.Copy, scale=SCALE).then_inc(S["hi_done"], 1)

            for t in range(TILES + 2):
                gnn_tile(t, t % 2)

            for h in range(2):
                act.wait_ge(listed[h], 32 * (TILES // 2))

            def load_entries(i):
                row = 0 if isinstance(i, int) and i == 0 else act.value_load(
                    ftab[0:1, 1, i:i + 1] if isinstance(i, int) else ftab[0:1, 1, bass.ds(i, 1)], min_val=0,
                    max_val=DUMP + 3 * P)
                if not (isinstance(i, int) and i == 0):
                    act.wait_ge(S["ents_in"], 16 * i)
                act.dma_start(ents[:, bass.ds(i & 7, 1), :].rearrange("p a n -> p (a n)"), lists[bass.ds(row, P), :]
                              ).then_inc(S["ents_in"], 16)

            load_entries(0)
            act.wait_ge(S["table_done"], 1)
            last = act.value_load(last_tile[0:1, E - 1:E], min_val=E - 1, max_val=TILES_MAX - 1)
            for i in range(1, 4):
                load_entries(i)

            def gelu(i):
                act.wait_ge(S["hsum_done"], i + 1)
                act.activation(hgelu, hsum, ACT.Gelu).then_inc(S["gelu_done"], 1)
                act.wait_ge(S["gelu_done"], i + 1)
                act.copy(hsplit[:, 0, :], hgelu).then_inc(S["hhi_done"], 1)

            def gated(i):
                act.wait_ge(S["ysum_done"], i + 1)
                if not (isinstance(i, int) and i == 0):
                    act.wait_ge(S["y_added"], 16 * i)
                act.activation(yout, ysum, ACT.Copy,
                               scale=ents[:, bass.ds(i & 7, 1), 2:3].rearrange("p a n -> p (a n)").bitcast(F32)
                               ).then_inc(S["y_done"], 1)

            def split_high_units(e, units):
                for u in units:
                    act.wait_ge(unit_in[u], 16 * e + (48 if u < RING else 16))
                    to = slots[:, bass.ds((e + 1) & 1, 1), 0, u, :].rearrange("p a n -> p (a n)")
                    act.activation(to, staging[:, u, :], ACT.Copy, scale=SCALE).then_inc(S["hi_done"], 1)

            gelu(0)
            split_high_units(0, range(RING))
            with act.Fori(0, last) as i:
                e, _, first_tile = experts_of(act, i)
                gelu(i + 1)
                with act.If(first_tile):
                    split_high_units(e, range(RING, UNITS))
                load_entries(i + 4)
                e_next, _, first_next = experts_of(act, i + 1)
                act.wait_ge(S["l2_done"], i + 1)
                act.sem_inc(S["act_passed"], 1)
                with act.If(first_next):
                    split_high_units(e_next, range(RING))
                gated(i)
            gated(last)
            act.wait_ge(S["ents_in"], 16 * (last + 4))
            act.sem_inc(S["act_passed"], 1)

        @block.vector
        def _(dve):
            c_edge = Chain(dve, S["c_edge"], 10 ** 6)
            c_rng = Chain(dve, S["c_rng"], 10 ** 6)
            c_tab = Chain(dve, S["c_tab"], 10 ** 6)
            c_ln = Chain(dve, S["c_ln"], 16)
            c_rt = Chain(dve, S["c_rt"], 11)
            c_rk = Chain(dve, S["c_rk"], 5)

            def bn(src_tile, kind):
                for b in range(2):
                    c_ln.inc(dve.bn_stats(bn6[:, kind, b, :], src_tile[:, b * HALF:(b + 1) * HALF]))

            def scales(first, kinds, scale, bias):
                k = slice(first, first + kinds)
                dve.wait_ge(S["c_ln"], c_ln.base + c_ln.n)
                dve.sem_inc(S["dve_passed"], 1)
                for kind in range(first, first + kinds):
                    c_ln.inc(dve.bn_aggr(mv[:, kind, :], bn6[:, kind]))
                dve.wait_ge(S["c_ln"], c_ln.base + c_ln.n)
                m, y, z, q = (nwt[:, j, k] for j in range(4))
                c_ln.link(dve.tensor_scalar(m, mv[:, k, 1], EPS, None, ALU.add))
                c_ln.link(dve.tensor_scalar(y.bitcast(I32), m.bitcast(I32), -0.5, float(MAGIC), ALU.mult, ALU.add))
                c_ln.link(dve.tensor_tensor(z, m, y, ALU.mult))
                for three in (3.0, 12.0, 768.0):
                    c_ln.link(dve.tensor_tensor(q, z, y, ALU.mult))
                    if three < 768.0:
                        c_ln.inc(dve.scalar_tensor_tensor(z, q, -three, z, ALU.add, ALU.mult))
                    c_ln.link(dve.scalar_tensor_tensor(y, q, -three, y, ALU.add, ALU.mult))
                dve.tensor_scalar(scale, y, -1.0 / 8192, None, ALU.mult)
                dve.scalar_tensor_tensor(bias, mv[:, k, 0], 1.0 / 8192, y, ALU.mult, ALU.mult
                                         ).then_inc(S["stats_done"], 1)
                dve.sem_inc(S["c_ln"], c_ln.per - c_ln.n)
                c_ln.n = c_ln.per

            c_ln.start(0)
            for h in range(2):
                dve.wait_ge(x_in[h], 16)
                bn(xin[:, h, :], h)
            scales(0, 2, ab0[:, :, 0], ab0[:, :, 1])

            L = c_edge.link
            dve.wait_ge(S["edges_in"], 16 * 9)
            dve.wait_ge(S["k32_in"], 16)
            c_edge.start(0)
            L(dve.tensor_scalar(tmp_i, edge_i[:, :, 1, :], 6, None, ALU.arith_shift_right))
            L(dve.tensor_copy(quant[:, :, 0, :], tmp_i))
            L(dve.tensor_scalar(tmp_i, edge_i[:, :, 1, :], WIN - 1, None, ALU.bitwise_and))
            c_edge.inc(dve.tensor_copy(quant[:, :, 1, :], tmp_i))
            c_edge.inc(dve.tensor_scalar(quant[:, :, 2, :], edge_i[:, :, 0, :], 1.0, None, ALU.add))
            L(dve.tensor_scalar(quant[:, :, 3, :], edge_f, SCALE, None, ALU.mult))
            dve.engine_nop().then_inc(S["quant_done"], 1)
            R = c_rng.link
            c_rng.start(0)
            c_rng.inc(dve.tensor_reduce(bmm[:, 0, :], quant[:, :, 0, :], AX.X, ALU.min))
            R(dve.tensor_reduce(bmm[:, 1, :], quant[:, :, 0, :], AX.X, ALU.max))
            wi = k32[:, S_I16:S_I16 + WINS]
            for h in range(2):
                R(dve.tensor_scalar(touch[:, h, 0, :], wi, bmm[:, 0, h:h + 1], None, ALU.is_ge))
                R(dve.scalar_tensor_tensor(touch[:, h, 1, :], wi, bmm[:, 1, h:h + 1], touch[:, h, 0, :], ALU.is_le, ALU.mult))
                R(dve.tensor_scalar(touch[:, h, 0, :], touch[:, h, 1, :], k32[:, S_CH + h:S_CH + h + 1], -BIG,
                                    ALU.mult, ALU.add))
                R(dve.tensor_scalar(touch[:, h, 1, :], touch[:, h, 1, :], k32[:, S_CH + 2 + h:S_CH + 3 + h], None, ALU.mult))
            R(dve.tensor_tensor(lohi[:].rearrange("p (a w) -> p a w", a=2), touch[:, 0], touch[:, 1], ALU.max))
            dve.engine_nop().then_inc(S["range_done"], 1)
            dve.wait_ge(S["edges_turned"], 1)
            L(dve.tensor_copy(eT, psA[:].rearrange("p a n -> p (a n)").rearrange("p (q n) -> p q n", q=4)))
            L(dve.tensor_copy(whi16[:], eT[:, 3, :]))
            L(dve.tensor_copy(whl[:, 0, :], whi16[:]))
            L(dve.tensor_tensor(whl[:, 1, :], eT[:, 3, :], whl[:, 0, :], ALU.subtract))
            dve.engine_nop().then_inc(S["parts_done"], 1)
            shape = [P, NCH, WIN]
            dve.tensor_tensor(dst1h, eT[:, 1, 0:NCH].unsqueeze(2).to_broadcast(shape),
                              k32[:, S_I64:S_I64 + WIN].unsqueeze(1).to_broadcast(shape), ALU.is_equal
                              ).then_inc(S["dst1h_done"], 1)

            filled = [0]

            def R(ins):
                c_rng.inc(ins)
                w = filled[0]
                if w < WINS:
                    c_edge.inc(dve.scalar_tensor_tensor(srcw[:, w, :], eT[:, 0, 0:NCH], float(w), eT[:, 2, 0:NCH],
                                                        ALU.is_equal, ALU.mult))
                    filled[0] += 1
                dve.wait_ge(S["c_rng"], c_rng.base + c_rng.n)

            dve.wait_ge(S["range_turned"], 1)
            R(dve.tensor_reduce(lohiT[:], psT[0:2 * WINS, 0].rearrange("p a n -> p (a n)").bitcast(F32)[:, 0:P], AX.X, ALU.max))
            dve.engine_nop().then_inc(S["range_row"], 1)
            dve.wait_ge(S["range_turned"], 2)
            R(dve.tensor_copy(wrow[:, 0:2, :].rearrange("p a w -> p (a w)"),
                              psT[0:1, 1].rearrange("p a n -> p (a n)").bitcast(F32)[:, 0:2 * WINS]))
            R(dve.scalar_tensor_tensor(wrow[:, 2, :], wrow[:, 0, :], -1.0, wrow[:, 1, :], ALU.mult, ALU.min))
            R(dve.tensor_scalar(wrow[:, 2, :], wrow[:, 2, :], float(NCH - LEAST * GRP), None, ALU.min))
            R(dve.tensor_tensor(wrow[:, 3, :], wrow[:, 1, :], wrow[:, 2, :], ALU.subtract))
            R(dve.tensor_scalar(wrow[:, 3, :], wrow[:, 3, :], float(GRP - 1), None, ALU.add))
            R(dve.tensor_copy(wtab[:, 0:2, :], wrow[:, 2:4, :]))
            R(dve.tensor_scalar(wtab[:, 1, :], wtab[:, 1, :], 2, None, ALU.arith_shift_right))
            R(dve.tensor_scalar(wtab[:, 1, :], wtab[:, 1, :], float(LEAST), None, ALU.max))
            R(dve.tensor_copy(wrow[:, 3, :], wtab[:, 1, :]))
            R(dve.memset(wrow[:, 5, :], 1.0))
            R(dve.tensor_tensor_scan(wrow[:, 4, :], wrow[:, 5, :], wrow[:, 3, :], 0.0, ALU.mult, ALU.add))
            R(dve.tensor_tensor(wtab[:, 2, :], wrow[:, 4, :], wrow[:, 3, :], ALU.subtract))
            R(dve.scalar_tensor_tensor(wtab[:, 4, :], wtab[:, 1, :], float(GRP), wtab[:, 0, :], ALU.mult, ALU.add))
            R(dve.tensor_scalar(wtab[:, 4, :], wtab[:, 4, :], float(GRP - 1), None, ALU.add))
            R(dve.tensor_scalar(wtab[:, 4, :], wtab[:, 4, :], 2, None, ALU.arith_shift_right))
            R(dve.tensor_copy(wrow[:, 3, :], wtab[:, 4, :]))
            R(dve.tensor_tensor_scan(wrow[:, 4, :], wrow[:, 5, :], wrow[:, 3, :], 0.0, ALU.mult, ALU.max))
            R(dve.memset(wtab[:, 3, 0:1], 0))
            R(dve.tensor_copy(wtab[:, 4, :], wrow[:, 4, :]))
            R(dve.tensor_copy(wtab[:, 3, 1:WINS], wrow[:, 4, 0:WINS - 1]))
            R(dve.scalar_tensor_tensor(wpack[:, 0, :], wtab[:, 2, :], 2.0 ** 8, wtab[:, 0, :], ALU.mult, ALU.add))
            R(dve.scalar_tensor_tensor(wpack[:, 0, :], wpack[:, 0, :], 2.0 ** 6, wtab[:, 1, :], ALU.mult, ALU.add))
            R(dve.scalar_tensor_tensor(wpack[:, 1, :], wtab[:, 3, :], 2.0 ** 6, wtab[:, 4, :], ALU.mult, ALU.add))
            dve.engine_nop().then_inc(S["wtab_done"], 1)
            assert filled[0] == WINS
            dve.wait_ge(S["c_edge"], c_edge.base + c_edge.n)
            dve.wait_ge(S["consts_in"], 32)
            def onehots(g, w, c):
                hot4 = ring1h[:, bass.ds(GRP * (g & 1), GRP), :]
                src4 = srcw_flat[:, bass.ds(w * NCH + c, GRP)]
                for k in range(GRP):
                    dve.wait_ge(src1h_used[k], g + 1)
                    dve.tensor_scalar(hot4[:, k, :], iota1, src4[:, k:k + 1], None, ALU.is_equal
                                      ).then_inc(src1h_ready[k], 1)

            def window(w):
                first, groups, before = window_range(dve, w)
                for j in range(LEAST):
                    onehots(before + j, w, within(first + GRP * j, 0, NCH - GRP))
                with dve.If(groups > LEAST):
                    with dve.Fori(LEAST, groups) as j:
                        onehots(before + j, w, within(first + GRP * j, 0, NCH - GRP))

            with dve.Fori(0, WINS // 2) as i:
                window(2 * i)
                window(2 * i + 1)

            def copy_t1(t, h):
                dve.wait_ge(S["t1_done"], t + 1)
                if known(t, 2):
                    dve.wait_ge(S["gnn_done"], t - 1)
                dve.tensor_copy(xT[:, h], psT[:]).then_inc(S["t1_copied"], 1)

            copy_t1(0, 0)
            dve.wait_ge(S["brought"], WINS)
            dve.wait_ge(S["biases_in"], 16)
            c_tab.start(0)
            T_ = c_tab.link
            T_(dve.tensor_scalar(rws[:, :, 0:E], rw[:], SCALE, None, ALU.mult))
            T_(dve.scalar_tensor_tensor(rws[:, :, E:2 * E], rw[:], SCALE, rws[:, :, 0:E], ALU.mult, ALU.subtract))
            dve.engine_nop().then_inc(S["rws_done"], 1)


            c_tab.inc(dve.memset(cnts[:, 3, :], 1.0))

            def rank_slots(t, h):
                dve.wait_ge(S["rank_done"], t + 1)
                if known(t, 2):
                    dve.wait_ge(listed[h], 32 * (t // 2))
                c_rk.start(t)
                c_rk.inc(dve.tensor_copy(before[0:1, bass.ds(t, 1)], psK[0:1, E - 1:E]))
                c_rk.link(dve.tensor_tensor(pos[:, 0, :], psK[:, 0:E], k32[:, S_EB:S_EB + E], ALU.add))
                c_rk.inc(dve.tensor_tensor(pos[:, 1, :], pos[:, 0, :], pick[:, 0, :], ALU.mult))
                c_rk.link(dve.tensor_tensor(pos[:, 2, :], pos[:, 0, :], pick[:, 1, :], ALU.mult))
                c_rk.link(dve.tensor_reduce(slotf[:], pos[:, 1:3, :], AX.X, ALU.add))
                dve.tensor_tensor(slot_i[:, h, :], slotf[:], dump_cols(t), ALU.add).then_inc(S["slot_done"], 1)

            def dump_cols(t):
                return k32[:, bass.ds(2 * t + S_DUMP, 2)]

            def mask_col(t):
                return k32[:, bass.ds(t + S_MASK, 1)]

            def entry_cols(t):
                return kdest[:, bass.ds(4 * t, 4)].rearrange("p (c a) -> p c a", a=2)

            def route(t, h):
                dve.wait_ge(S["router_done"], t + 1)
                c_rt.start(t)
                K = c_rt.link
                K(dve.tensor_copy(logit[:, 0, :], psR[:, 0:E]))
                c_rt.link_apart(dve.tensor_tensor(logit[:, 1, :], logit[:, 0, :], psR[:, E:2 * E], ALU.add), S["dve_passed"])
                c_rt.link_apart(dve.max(m8[:], logit[:, 1, :]), S["dve_passed"])
                K(dve.max_index(i8[:], m8[:], logit[:, 1, :]))
                dve.tensor_scalar(nb[:], m8[:, 0:1], -1.0 / SCALE, None, ALU.mult).then_inc(S["nb_done"], 1)
                K(dve.tensor_copy(idf[:], i8[:, 0:2]))
                c_rt.inc(dve.tensor_scalar(pick[:, 0, :], k32[:, S_I8:S_I8 + E], idf[:, 0:1], mask_col(t), ALU.is_equal, ALU.mult))
                K(dve.tensor_scalar(pick[:, 1, :], k32[:, S_I8:S_I8 + E], idf[:, 1:2], mask_col(t), ALU.is_equal, ALU.mult))
                if known(t, 1):
                    dve.wait_ge(S["rank_done"], t)
                    dve.wait_ge(S["mask_done"], t)
                K(dve.tensor_tensor(mk[:, 0, :], pick[:, 0, :], pick[:, 1, :], ALU.add))
                dve.tensor_tensor(mcum[:, 1 - h, :], mcum[:, h, :], mk[:, 0, :], ALU.add).then_inc(S["mask_done"], 1)
                dve.wait_ge(S["exp_done"], t + 1)
                if known(t, 2):
                    dve.wait_ge(listed[h], 32 * (t // 2))
                c_rt.inc(dve.tensor_copy(ent[:, h, :, 0:2], entry_cols(t)))
                K(dve.tensor_scalar(gs[:], ex[:], 1.0, None, ALU.add))
                K(dve.reciprocal(ent[:, h, 0, 2:3].bitcast(F32), gs[:]))
                dve.tensor_tensor(ent[:, h, 1, 2:3].bitcast(F32), ex[:], ent[:, h, 0, 2:3].bitcast(F32), ALU.mult
                                  ).then_inc(S["gate_done"], 1)

            def low_unit(t):
                dve.wait_ge(S["hi_done"], t - 1)
                u = t - 2
                hi = slots[:, 0, 0, bass.ds(u, 1), :].rearrange("p a n -> p (a n)")
                lo = slots[:, 0, 1, bass.ds(u, 1), :].rearrange("p a n -> p (a n)")
                st = staging[:, bass.ds(u % RING, 1), :].rearrange("p a n -> p (a n)")
                dve.scalar_tensor_tensor(lo, st, SCALE, hi, ALU.mult, ALU.subtract).then_inc(S["lo_done"], 1)

            def residual(t, h):
                dve.wait_ge(S["gnn_done"], t + 1)
                dve.wait_ge(S["xb_done"], t + 1)
                if known(t, 2):
                    dve.wait_ge(x1_out[h], 16 * (t // 2))
                    dve.wait_ge(S["xln2_done"], t - 1)
                dve.scalar_tensor_tensor(x1[:, h, :], psG[h], 1.0 / SCALE, xb[:, h, :],
                                         ALU.mult, ALU.add).then_inc(S["x1_done"], 1)

            def gnn_tile(t, h):
                one, two = below(t, TILES - 2), known(t, 1) and below(t, TILES + 1)
                if two:
                    residual(t - 1, 1 - h)
                if one or two:
                    c_ln.start(t + 1)
                if one:
                    dve.wait_ge(x_in[h], 16 * (t // 2 + 2))
                    bn(xin[:, h, :], 0)
                if two:
                    dve.wait_ge(S["x1_done"], t)
                    bn(x1[:, 1 - h, :], 1)
                if known(t, 2):
                    dve.wait_ge(S["xln_done"], t if below(t, TILES) and not isinstance(t, int) else min(t, TILES))
                    dve.wait_ge(S["xln2_done"], t - 2 if below(t, TILES + 2) and not isinstance(t, int) else t - 2)
                if one or two:
                    first = 0 if one else 1
                    kinds = 2 if one and two else 1
                    scales(first, kinds, ab[:, h, 0, first:first + kinds], ab[:, h, 1, first:first + kinds])
                if known(t, 2) and below(t, TILES):
                    low_unit(t)
                if isinstance(t, int) and t == TILES + 1:
                    dve.wait_ge(S["t2_done"], TILES)
                    dve.wait_ge(S["router_done"], TILES - 1)
                    dve.tensor_copy(x2T[:, 1], psT[:, 1]).then_inc(S["low_copied"], 1)
                if known(t, 2):
                    route(t - 2, h)
                if below(t, TILES - 1):
                    copy_t1(t + 1, 1 - h)
                if known(t, 2):
                    rank_slots(t - 2, h)

            dve.wait_ge(S["mcum_zero"], 2)
            tiles(gnn_tile, dve)
            dve.wait_ge(S["count_done"], 1)
            counts = psR[0:1, 0:E]
            T_(dve.tensor_scalar(cnti[:], counts, float(P - 1), None, ALU.add))
            T_(dve.tensor_scalar(cnti[:], cnti[:], 7, None, ALU.arith_shift_right))
            T_(dve.tensor_scalar(cnts[:, 2, :], cnti[:], 1.0, None, ALU.max))
            T_(dve.tensor_tensor_scan(cnts[:, 4, :], cnts[:, 3, :], cnts[:, 2, :], 0.0, ALU.mult, ALU.add))
            c_tab.inc(dve.tensor_scalar(before[:, TILES:TILES + 1], counts[:, E - 1:E], 1.0, None, ALU.max))
            c_tab.inc(dve.tensor_scalar(last_tile[:], cnts[:, 4, :], -1.0, None, ALU.add))
            ti = k32[0:1, S_IT:S_IT + TMAX]
            T_(dve.tensor_tensor(tt[:, 0], ti.unsqueeze(2).to_broadcast([1, TMAX, E]),
                                 cnts[:, 4, :].unsqueeze(1).to_broadcast([1, TMAX, E]), ALU.is_ge))
            T_(dve.tensor_tensor(tt[:, 1], tt[:, 0], cnts[:, 2, :].unsqueeze(1).to_broadcast([1, TMAX, E]), ALU.mult))
            c_tab.inc(dve.tensor_reduce(tf[:, 0, :], tt[:, 0], AX.X, ALU.add))
            T_(dve.tensor_reduce(tf[:, 1, :], tt[:, 1], AX.X, ALU.add))
            c_tab.inc(dve.tensor_scalar(tf[:, 2, :], tf[:, 0, :], float(E - 1), None, ALU.min))
            T_(dve.tensor_tensor(tf[:, 3, :], ti, tf[:, 1, :], ALU.subtract))
            c_tab.inc(dve.tensor_scalar(tf[:, 5, :], tf[:, 3, :], 0.0, None, ALU.is_equal))
            T_(dve.tensor_scalar(tf[:, 4, :], tf[:, 3, :], float(P), None, ALU.mult))
            c_tab.inc(dve.scalar_tensor_tensor(tf[:, 5, :], tf[:, 2, :], float(E - 1), tf[:, 5, :], ALU.is_lt, ALU.mult))
            T_(dve.scalar_tensor_tensor(ftab[:, 1, :], tf[:, 2, :], float(CAP), tf[:, 4, :], ALU.mult, ALU.add))
            T_(dve.scalar_tensor_tensor(tf[:, 5, :], tf[:, 5, :], 8.0, tf[:, 2, :], ALU.mult, ALU.add))
            dve.scalar_tensor_tensor(ftab[:, 0, 0:TMAX - 1], tf[:, 2, 1:TMAX], 16.0, tf[:, 5, 0:TMAX - 1],
                                     ALU.mult, ALU.add).then_inc(S["table_done"], 1)
            T_(dve.tensor_scalar(needed[:], before[:, 1:TILES + 1], float(P - 1), None, ALU.add))
            T_(dve.tensor_scalar(needed[:], needed[:], 7, None, ALU.arith_shift_right))
            dve.tensor_scalar(needed[:], needed[:], cnts[:, 4, E - 2:E - 1], None, ALU.add).then_inc(S["needed_done"], 1)

            last = dve.value_load(last_tile[0:1, E - 1:E], min_val=E - 1, max_val=TILES_MAX - 1)

            def copy_rows(i):
                dve.wait_ge(S["xs_done"], i + 1)
                dve.tensor_copy(xsT, psT[:]).then_inc(S["xsT_copied"], 1)

            def sum_h(i, e):
                dve.wait_ge(S["l1_done"], i + 1)
                dve.wait_ge(S["ffn_bias_in"], 32 * e + 32)
                if not (isinstance(i, int) and i == 0):
                    dve.wait_ge(S["gelu_done"], i)
                bias1 = ffn_bias[:, bass.ds(e & 3, 1), 0:F].rearrange("p a n -> p (a n)")
                dve.scalar_tensor_tensor(hsum, psH, 1.0 / SCALE, bias1, ALU.mult, ALU.add).then_inc(S["hsum_done"], 1)

            def sum_y(i, e):
                dve.wait_ge(S["l2_done"], i + 1)
                if not (isinstance(i, int) and i == 0):
                    dve.wait_ge(S["y_done"], i)
                bias2 = ffn_bias[:, bass.ds(e & 3, 1), F:F + D].rearrange("p a n -> p (a n)")
                dve.scalar_tensor_tensor(ysum, psA[:].rearrange("p a n -> p (a n)"), 1.0 / SCALE, bias2,
                                         ALU.mult, ALU.add).then_inc(S["ysum_done"], 1)

            def split_h(i):
                dve.wait_ge(S["hhi_done"], i + 1)
                dve.tensor_tensor(hsplit[:, 1, :], hgelu, hsplit[:, 0, :], ALU.subtract).then_inc(S["hlo_done"], 1)

            def copy_h(i):
                dve.wait_ge(S["ht_done"], i + 1)
                dve.tensor_copy(hT[:, :, 0:FB, :], psHT).then_inc(S["ht_copied"], 1)

            copy_rows(0)
            sum_h(0, 0)
            copy_rows(1)
            split_h(0)
            copy_h(0)
            def next_weights(e, first_tile, units):
                with dve.If(first_tile):
                    for u in units:
                        dve.wait_ge(S["hi_done"], UNITS * (e + 1) + u + 1)
                        base = slots[:, bass.ds((e + 1) & 1, 1), :, u, :].rearrange("p a s n -> p (a s) n")
                        dve.scalar_tensor_tensor(base[:, 1, :], staging[:, u, :], SCALE, base[:, 0, :],
                                                 ALU.mult, ALU.subtract).then_inc(S["lo_done"], 1)

            with dve.Fori(0, last) as i:
                e0, e1, first_tile = experts_of(dve, i)
                next_weights(e0, first_tile, range(RING))
                sum_h(i + 1, e1)
                copy_rows(i + 2)
                split_h(i + 1)
                next_weights(e0, first_tile, range(RING, RING + 2))
                sum_y(i, e0)
                copy_h(i + 1)
                next_weights(e0, first_tile, range(RING + 2, UNITS))
            sum_y(last, E - 1)

        @block.tensor
        def _(pe):
            pe.wait_ge(S["quant_done"], 1)
            turned = psA[:].rearrange("p a n -> p (a n)").rearrange("p (q h n) -> p q h n", q=4, h=2)
            for q in range(4):
                for h in range(2):
                    ins = pe.transpose(turned[:, q, h, :], quant[:, h, q, :], ident32)
            ins.then_inc(S["edges_turned"], 1)
            pe.wait_ge(S["range_done"], 1)
            pe.transpose(psT[0:2 * WINS, 0].rearrange("p a n -> p (a n)").bitcast(F32)[:, 0:P], lohi[:], ident32
                         ).then_inc(S["range_turned"], 1)
            pe.wait_ge(S["range_row"], 1)
            pe.transpose(psT[0:1, 1].rearrange("p a n -> p (a n)").bitcast(F32)[:, 0:2 * WINS], lohiT[:],
                         ident32[0:2 * WINS, 0:2 * WINS]).then_inc(S["range_turned"], 1)
            for k in range(GRP):
                pe.sem_inc(src1h_used[k], 2)
            pe.wait_ge(S["wtab_done"], 1)

            def turn(rows, out_t, done):
                for part in range(2):
                    for k in range(KB):
                        ins = pe.transpose(out_t[:, part, k, :], rows[:, part * D + k * P:part * D + (k + 1) * P], ident)
                ins.then_inc(done, 1)

            def turn1(t, h):
                pe.wait_ge(S["lo1_done"], t + 1)
                if known(t, 1):
                    pe.wait_ge(S["t1_copied"], t)
                if known(t, 3):
                    pe.wait_ge(S["t2_copied"], t - 2)
                turn(row1[:, h, :], psT, S["t1_done"])

            def group(g, c, h, start):
                st4 = stat[:, bass.ds(c, GRP), :]
                hot4 = ring1h[:, bass.ds(GRP * (g & 1), GRP), :]
                pe.wait_ge(S["stat_hi_done"], c + GRP)
                pe.wait_ge(S["stat_lo_done"], c + GRP)
                for k in range(GRP):
                    pe.wait_ge(src1h_ready[k], g + 1)
                    st, hot = st4[:, k, :], hot4[:, k, :]
                    for b in range(2):
                        ins = pe.matmul(psW[:, 2 * h + b, :], st, hot[:, b * HALF:(b + 1) * HALF],
                                        start=(start and k == 0), stop=False, skip_group_check=True)
                    ins.then_inc(src1h_used[k], 1)

            def window(w, h):
                first, groups, before = window_range(pe, w)
                if not isinstance(w, int):
                    pe.wait_ge(S["brought"], w - 1)
                for j in range(LEAST):
                    group(before + j, within(first + GRP * j, 0, NCH - GRP), h, j == 0)
                with pe.If(groups > LEAST):
                    with pe.Fori(LEAST, groups) as j:
                        group(before + j, within(first + GRP * j, 0, NCH - GRP), h, False)

            pe.wait_ge(S["consts_in"], 32)
            turn1(0, 0)
            window(0, 0)
            window(1, 1)
            with pe.Fori(1, WINS // 2) as i:
                window(2 * i, 0)
                window(2 * i + 1, 1)

            def rank(t, h):
                pe.wait_ge(S["mask_done"], t + 1)
                if known(t, 1):
                    pe.wait_ge(S["slot_done"], t)
                pe.matmul(psK[:, 0:E], tri, mk[:, 0, :], start=True, stop=False)
                pe.matmul(psK[:, 0:E], ones, mcum[:, h, :], start=False, stop=True).then_inc(S["rank_done"], 1)

            def turn2(t, h):
                pe.wait_ge(S["lo2_done"], t + 1)
                pe.wait_ge(S["t1_copied"], t + 3 if below(t, TILES - 2) and not isinstance(t, int) else min(t + 3, TILES))
                if known(t, 1):
                    pe.wait_ge(S["t2_copied"], t)
                turn(row2[:, h, :], psT, S["t2_done"])

            def router_mm(t):
                pe.wait_ge(S["t2_copied"], t + 1)
                if isinstance(t, int) and t == TILES - 1:
                    pe.wait_ge(S["low_copied"], 1)
                if known(t, 1):
                    pe.wait_ge(S["mask_done"], t)
                for part in range(2):
                    for k in range(KB):
                        ins = pe.matmul(psR[:, 0:2 * E], x2T[:, part, k, :], rws[:, k, :],
                                        start=(part == 0 and k == 0), stop=(part == 1 and k == KB - 1))
                ins.then_inc(S["router_done"], 1)

            def products(t, h, blocks):
                for k in blocks:
                    for part, wpart in ((0, 0), (0, 1), (1, 0)):
                        for b in range(2):
                            ins = pe.matmul(psG[h][:, b * HALF:(b + 1) * HALF], xT[:, h, part, k, :],
                                            wT[:, wpart, k, b * HALF:(b + 1) * HALF],
                                            start=(k == 0 and part == 0 and wpart == 0), stop=(k == KB - 1 and part == 1))
                if blocks[-1] == KB - 1:
                    ins.then_inc(S["gnn_done"], 1)

            def gnn_tile(t, h):
                now = below(t, TILES)
                if now:
                    pe.wait_ge(S["t1_copied"], t + 1)
                    if known(t, 2):
                        pe.wait_ge(S["x1_done"], t - 1)
                    products(t, h, (0, 1))
                if known(t, 2):
                    turn2(t - 2, h)
                if now:
                    products(t, h, (2, 3))
                if known(t, 2):
                    router_mm(t - 2)
                if below(t, TILES - 1):
                    turn1(t + 1, 1 - h)
                if now:
                    products(t, h, (4, 5))
                if known(t, 2):
                    rank(t - 2, h)
                if isinstance(t, int) and t == 0:
                    pe.wait_ge(S["wsplit_done"], WINS // 2)
                    pe.wait_ge(S["rws_done"], 1)
                if now:
                    products(t, h, (6, 7))

            pe.wait_ge(S["wsplit_done"], WINS // 2 - 1)
            tiles(gnn_tile, pe)
            pe.wait_ge(S["mask_done"], TILES)
            pe.matmul(psR[:, 0:E], ones, mcum[:, 0, :], start=True, stop=True).then_inc(S["count_done"], 1)

            pe.wait_ge(S["table_done"], 1)
            last = pe.value_load(last_tile[0:1, E - 1:E], min_val=E - 1, max_val=TILES_MAX - 1)

            def turn_rows(i):
                pe.wait_ge(S["xs_in"], 16 * (i + 1))
                if not (isinstance(i, int) and i == 0):
                    pe.wait_ge(S["xsT_copied"], i)
                turn(xs, psT, S["xs_done"])

            def layer1(i, e):
                pe.wait_ge(S["xsT_copied"], i + 1)
                if not (isinstance(i, int) and i == 0):
                    pe.wait_ge(S["hsum_done"], i)
                pe.wait_ge(S["lo_done"], UNITS * e + RING)
                slot = slots[:, bass.ds(e & 1, 1)].rearrange("p o a b n -> p (o a) b n")
                for k in range(KB):
                    cols = slice((k % 2) * F, (k % 2) * F + F)
                    for part, wpart in ((0, 0), (0, 1), (1, 0)):
                        ins = pe.matmul(psH, xsT[:, part, k, :], slot[:, wpart, k // 2, cols],
                                        start=(k == 0 and part == 0 and wpart == 0), stop=(k == KB - 1 and part == 1))
                ins.then_inc(S["l1_done"], 1)

            def turn_h(i):
                pe.wait_ge(S["hlo_done"], i + 1)
                if not (isinstance(i, int) and i == 0):
                    pe.wait_ge(S["ht_copied"], i)
                for part in range(2):
                    for f in range(FB):
                        ins = pe.transpose(psHT[:, part, f, :], hsplit[:, part, f * P:(f + 1) * P], ident)
                ins.then_inc(S["ht_done"], 1)

            def layer2(i, e):
                pe.wait_ge(S["ht_copied"], i + 1)
                if not (isinstance(i, int) and i == 0):
                    pe.wait_ge(S["ysum_done"], i)
                pe.wait_ge(S["lo_done"], UNITS * e + UNITS)
                slot = slots[:, bass.ds(e & 1, 1)].rearrange("p o a b n -> p (o a) b n")
                for f in range(FB):
                    for part, wpart in ((0, 0), (0, 1), (1, 0)):
                        for b in range(2):
                            ins = pe.matmul(psA[:, b, :], hT[:, part, f, :], slot[:, wpart, 4 + f, b * HALF:(b + 1) * HALF],
                                            start=(f == 0 and part == 0 and wpart == 0),
                                            stop=(f == FB - 1 and part == 1))
                ins.then_inc(S["l2_done"], 1)

            turn_rows(0)
            layer1(0, 0)
            turn_rows(1)
            turn_h(0)
            with pe.Fori(0, last) as i:
                e0, e1, _ = experts_of(pe, i)
                layer1(i + 1, e1)
                turn_rows(i + 2)
                layer2(i, e0)
                turn_h(i + 1)
            layer2(last, E - 1)


def constants(np):
    p = np.arange(P)
    k16 = np.zeros((P, H_END), np.float16)
    k16[:, H_ID:H_ID + P] = np.eye(P)
    k16[:, H_TRI:H_TRI + P] = p[:, None] < p[None, :]
    k16[:, H_ONE:H_ONE + P] = 1
    k16[:, H_IOTA:H_IOTA + D] = np.arange(1, D + 1)
    k32 = np.zeros((P, S_END), np.float32)
    k32[:, S_ID:S_ID + P] = np.eye(P)
    k32[:, S_I64:S_I64 + WIN] = np.arange(WIN)
    k32[:, S_I16:S_I16 + WINS] = np.arange(WINS)
    k32[:, S_I8:S_I8 + E] = np.arange(E)
    for h in range(2):
        k32[:, S_CH + h] = BIG - (p + P * h)
        k32[:, S_CH + 2 + h] = p + P * h + 1
    k32[:, S_EB:S_EB + E] = np.arange(E) * CAP
    k32[:, S_MASK:S_MASK + TILES] = 1
    k32[:REPEAT, S_MASK + TILES - 1] = 0
    for c in range(2):
        k32[:REPEAT, S_DUMP + 2 * (TILES - 1) + c] = DUMP + P * c + p[:REPEAT]
    k32[:, S_IT:S_IT + TMAX] = np.arange(TMAX)
    kd = np.zeros((P, TILES, 2, 2), np.int32)
    for t in range(TILES):
        kd[:, t] = (min(P * t, LAST) + p)[:, None, None]
    kd = kd.reshape(P, 4 * TILES)
    pads = np.zeros((DUMP + 4 * P, 4), np.int32)
    pads[:, 1] = N + np.arange(DUMP + 4 * P) % P
    return k16, k32, kd, pads


def kernel(x, src, dst, edge_weight, L0_gnn_bias, L0_ffn_router_w, L0_ffn_w1, L0_ffn_b1, L0_ffn_w2, L0_ffn_b2):
    import numpy as np
    import concourse.bacc as bacc
    from concourse.bass_utils import run_bass_kernel_spmd

    def lay(a):
        return np.ascontiguousarray(a)

    k16, k32, kd, pads = constants(np)
    w1 = np.asarray(L0_ffn_w1).transpose(0, 2, 1).reshape(E, UNITS // 2, 2, P, F).transpose(0, 1, 3, 2, 4)
    w2 = np.asarray(L0_ffn_w2).transpose(0, 2, 1)
    arrays = {
        "x": lay(x), "src": lay(src), "dst": lay(dst), "edge_w": lay(edge_weight),
        "bias": lay(np.asarray(L0_gnn_bias).reshape(1, D)),
        "router": lay(np.asarray(L0_ffn_router_w).reshape(E, KB, P).transpose(2, 1, 0)),
        "w1u": lay(w1.reshape(E * UNITS // 2, P, 2 * F)), "w2u": lay(w2.reshape(E * FB, P, D)),
        "b1": lay(L0_ffn_b1), "b2": lay(L0_ffn_b2),
        "c16": k16, "c32": k32, "ci": kd, "cl": pads,
    }
    nc = bacc.Bacc("TRN2", target_bir_lowering=False, num_devices=1)
    args = {name: nc.dram_tensor(name, a.shape, mybir.dt.from_np(a.dtype), kind="ExternalInput").ap()
            for name, a in arrays.items()}
    out = nc.dram_tensor("out", (N, D), F32, kind="ExternalOutput").ap()
    build_program(nc, out=out, **args)
    r = run_bass_kernel_spmd(nc, [arrays], core_ids=[0])
    return r.results[0]["out"]
```
